# Optimizing a Trainium2 kernel written in Bass

```python
import numpy as np
import jax
import jax.numpy as jnp

def _softmax(x, axis=-1):
    return jax.nn.softmax(x, axis=axis)

def _gelu(x):
    return jax.nn.gelu(x, approximate=True)

def _silu(x):
    return jax.nn.silu(x)

def _sigmoid(x):
    return jax.nn.sigmoid(x)

def _layernorm(x, axis=-1, eps=1e-05):
    m = jnp.mean(x, axis=axis, keepdims=True)
    v = jnp.var(x, axis=axis, keepdims=True)
    return (x - m) / jnp.sqrt(v + eps)

def _scatter_add(tgt, idx, src, axis=0):
    return tgt.at[idx].add(src)

def _segment_sum(src, seg, n):
    return jax.ops.segment_sum(src, seg, n)
kernel_name = 'mk_seq_postln_d1_jaxref_r8_2de4f1'

def setup_inputs(seed: int=0):
    np.random.seed(seed)
    _w = jnp.asarray

    def _L0_attn_setup():
        import jax, jax.numpy as jnp
        import numpy as np
        B, S, D = (8, 512, 128)
        H, DK, DV, L = (8, 64, 64, 32)
        key = jax.random.key(seed)
        ks = jax.random.split(key, 6)
        x = jax.random.normal(ks[0], (B, S, D), dtype=jnp.float32)
        sd = 1.0 / np.sqrt(D)
        Wq = jax.random.normal(ks[1], (D, H * DK), dtype=jnp.float32) * sd
        Wk = jax.random.normal(ks[2], (D, H * DK), dtype=jnp.float32) * sd
        Wv = jax.random.normal(ks[3], (D, H * DV), dtype=jnp.float32) * sd
        betas = jax.random.normal(ks[4], (1, H, 1, DV), dtype=jnp.float32)
        Wo = jax.random.normal(ks[5], (H * DV, D), dtype=jnp.float32) * (1.0 / np.sqrt(H * DV))
        return {'x': x, 'Wq': Wq, 'Wk': Wk, 'Wv': Wv, 'betas': betas, 'Wo': Wo}
    _L0_attn_in = _L0_attn_setup()

    def _L0_ffn_setup():
        import jax, jax.numpy as jnp
        import numpy as np
        B, S, H, F, E = (4, 256, 128, 512, 8)
        key = jax.random.key(seed)
        ks = jax.random.split(key, 8)
        s = 1.0 / np.sqrt(H)
        sf = 1.0 / np.sqrt(F)
        return {'x': jax.random.normal(ks[0], (B, S, H), jnp.float32), 'wr': jax.random.uniform(ks[1], (H, E), jnp.float32, -s, s), 'br': jax.random.uniform(ks[2], (E,), jnp.float32, -s, s), 'w1': jax.random.uniform(ks[3], (E, H, F), jnp.float32, -s, s), 'b1': jax.random.uniform(ks[4], (E, F), jnp.float32, -s, s), 'w2': jax.random.uniform(ks[5], (E, F, H), jnp.float32, -sf, sf), 'b2': jax.random.uniform(ks[6], (E, H), jnp.float32, -sf, sf)}
    _L0_ffn_in = _L0_ffn_setup()
    _d = {'L0_attn_x': _L0_attn_in['x'], 'L0_attn_Wq': _L0_attn_in['Wq'], 'L0_attn_Wk': _L0_attn_in['Wk'], 'L0_attn_Wv': _L0_attn_in['Wv'], 'L0_attn_betas': _L0_attn_in['betas'], 'L0_attn_Wo': _L0_attn_in['Wo'], 'L0_ffn_wr': _L0_ffn_in['wr'], 'L0_ffn_br': _L0_ffn_in['br'], 'L0_ffn_w1': _L0_ffn_in['w1'], 'L0_ffn_b1': _L0_ffn_in['b1'], 'L0_ffn_w2': _L0_ffn_in['w2'], 'L0_ffn_b2': _L0_ffn_in['b2']}
    _x0 = _d['L0_attn_x']
    _d['L0_attn_x'] = jax.random.normal(jax.random.fold_in(jax.random.key(seed), 1), (1, 2048, 128), dtype=_x0.dtype)
    del _x0
    return _d

def reference(L0_attn_x, L0_attn_Wq, L0_attn_Wk, L0_attn_Wv, L0_attn_betas, L0_attn_Wo, L0_ffn_wr, L0_ffn_br, L0_ffn_w1, L0_ffn_b1, L0_ffn_w2, L0_ffn_b2):

    def _L0_attn_ref(x, Wq, Wk, Wv, betas, Wo):
        import jax, jax.numpy as jnp
        import numpy as np
        B, S, D = (8, 512, 128)
        H, DK, DV, L = (8, 64, 64, 32)
        b, s, d = x.shape
        n_seq = s // L
        xs = x.reshape(b, n_seq, L, d)

        def proj(W, dh):
            p = xs @ W
            return p.reshape(b, n_seq, L, H, dh).transpose(1, 0, 3, 2, 4)
        q = proj(Wq, DK)
        k = proj(Wk, DK)
        v = proj(Wv, DV)
        scale = 1.0 / np.sqrt(DK)
        gate = jax.nn.sigmoid(betas)
        mem0 = jnp.zeros((b, H, DK, DV), dtype=x.dtype)
        z0 = jnp.ones((b, H, DK, 1), dtype=x.dtype) / DK

        def step(carry, inp):
            mem, z = carry
            q_s, k_s, v_s = inp
            sq = jax.nn.elu(q_s) + 1.0
            att_mem = sq @ mem / (sq @ z)
            sk = jax.nn.elu(k_s) + 1.0
            mem = mem + jnp.einsum('bhlk,bhlv->bhkv', sk, v_s)
            z = z + sk.sum(axis=-2, keepdims=True).transpose(0, 1, 3, 2)
            att_dot = jax.nn.softmax(jnp.einsum('bhik,bhjk->bhij', q_s, k_s) * scale, axis=-1)
            att = att_dot @ v_s
            att = gate * att_mem + (1.0 - gate) * att
            return ((mem, z), att)
        _, outs = jax.lax.scan(step, (mem0, z0), (q, k, v))
        out = outs.transpose(1, 0, 3, 2, 4).reshape(b, s, H * DV)
        return out @ Wo

    def _L0_ffn_ref(x, wr, br, w1, b1, w2, b2):
        import jax, jax.numpy as jnp
        import numpy as np
        B, S, H, F, E = (4, 256, 128, 512, 8)
        scores = jnp.einsum('bsh,he->bse', x, wr) + br
        expert_id = jnp.argmax(scores, axis=-1)
        h = jnp.einsum('bsh,ehf->ebsf', x, w1) + b1[:, None, None, :]
        h = jax.nn.gelu(h, approximate=False)
        y = jnp.einsum('ebsf,efh->ebsh', h, w2) + b2[:, None, None, :]
        one_hot = jax.nn.one_hot(expert_id, E, dtype=x.dtype)
        out = jnp.einsum('ebsh,bse->bsh', y, one_hot)
        return out
    x = L0_attn_x
    x = _layernorm(x + _L0_attn_ref(x, L0_attn_Wq, L0_attn_Wk, L0_attn_Wv, L0_attn_betas, L0_attn_Wo), axis=-1)
    x = _layernorm(x + _L0_ffn_ref(x, L0_ffn_wr, L0_ffn_br, L0_ffn_w1, L0_ffn_b1, L0_ffn_w2, L0_ffn_b2), axis=-1)
    return x

_drawn_inputs = setup_inputs


def setup_inputs(seed=0):
    import zlib

    import numpy as np

    out = dict(_drawn_inputs(seed))
    spreads = {}
    factors = {'L0_ffn_b1': 3.144}
    for name, (base, spread) in spreads.items():
        noise = np.random.default_rng([zlib.crc32(name.encode()), seed]).standard_normal(out[name].shape)
        drawn = base * np.exp(spread * noise) if base else spread * noise
        out[name] = jnp.asarray(drawn.astype(out[name].dtype))
    for name, factor in factors.items():
        out[name] = (out[name] * factor).astype(out[name].dtype)
    return out
```

```python
from contextlib import ExitStack

import concourse.bass as bass
from concourse import mybir

ALU = mybir.AluOpType
ACT = mybir.ActivationFunctionType
AX_X = mybir.AxisListType.X
F32 = mybir.dt.float32
I32 = mybir.dt.int32
U32 = mybir.dt.uint32

P = 128
EPS = 1e-5


def build_program(nc, x, wq, wk, wv, betas, wo, wr, br, w1, b1, w2, b2, out):
    _, S, D = x.shape
    H, DV = betas.shape[1], betas.shape[3]
    DK = wq.shape[1] // H
    L = 32
    E, _, F = w1.shape
    NT = S // P
    NP = H // 2
    HD = H * DV
    FC = F // P
    V1 = DV + 1
    NS = (S + E * (P - 1)) // P
    ROW = D + 1
    REGION = S
    DUMMY = E * REGION
    SCALE = 1.0 / float(DK) ** 0.5
    W1P = F + FC
    W2P = FC * D + D
    assert D == P and 2 * DK == P and DK == DV and P == 4 * L and HD == 512 and F == 512 and NT % 2 == 0
    assert S < 4096 and NS % 2 == 1

    routed = nc.dram_tensor("routed_rows", [DUMMY + P, ROW], F32).ap()

    with ExitStack() as ctx:
        def sb(name, shape, dt=F32):
            return ctx.enter_context(nc.sbuf_tensor(name, shape, dt))

        def sem(name):
            return ctx.enter_context(nc.semaphore(name))

        x_sb = sb("x_sb", [P, NT * D])
        wq_sb, wk_sb, wv_sb = sb("wq_sb", [P, 512]), sb("wk_sb", [P, 512]), sb("wv_sb", [P, 512])
        wo_sb = sb("wo_sb", [P, NP, D])
        wr_sb = sb("wr_sb", [P, E])
        w1_sb = sb("w1_sb", [P, E * W1P])
        w2_sb = sb("w2_sb", [P, E * W2P])
        w1_v = w1_sb[:, :].rearrange("p (e n) -> p e n", e=E)
        w2_v = w2_sb[:, :].rearrange("p (e n) -> p e n", e=E)
        rows_sb = sb("rows_sb", [1, HD + E * D + E])
        gates_sb = sb("gates_sb", [1, 2 * HD])
        b1_rows = sb("b1_rows", [E * FC, P])
        gate, ungate = sb("gate", [P, HD]), sb("ungate", [P, HD])
        br_bc = sb("br_bc", [P, E])
        ident = sb("ident", [P, P])
        ones = sb("ones", [P, P])
        before = sb("before", [P, P])
        mask = sb("mask", [P, P])
        ids_i = sb("ids_i", [P, NT], I32)
        e_i = sb("e_i", [P, E], I32)
        e_f = sb("e_f", [P, E])
        base_f = sb("base_f", [P, E])
        fill = sb("fill", [P, NT, ROW], I32)
        xin = sb("xin", [P, 2, D])
        xT = sb("xT", [P, 2, P])
        qT, kT = sb("qT", [P, 2, NP, P]), sb("kT", [P, 2, NP, P])
        sqT, skT = sb("sqT", [P, 2, NP, P]), sb("skT", [P, 2, NP, P])
        q_exp, q_relu = sb("q_exp", [P, HD]), sb("q_relu", [P, HD])
        k_exp, k_relu = sb("k_exp", [P, HD]), sb("k_relu", [P, HD])
        sk = sb("sk", [P, 2, HD])
        vg, vu = sb("vg", [P, 2, H, V1]), sb("vu", [P, 2, H, DV])
        aT = sb("aT", [P, 2, H, P])
        mem = sb("mem", [P, 2, NP, 2 * V1])
        sl, pe_, pn = sb("sl", [P, 2, H, L]), sb("pexp", [P, 2, H, L]), sb("pnorm", [P, 2, H, L])
        pT = sb("pT", [P, 2, H, P])
        smax, rowsum, rrow = sb("smax", [P, H]), sb("rowsum", [P, H]), sb("rrow", [P, H])
        den, pscale = sb("den", [P, H]), sb("pscale", [P, H])
        rden = sb("rden", [P, 2, H])
        att = sb("att", [P, 2, HD])
        attT = sb("attT", [P, 2, NP, P])
        resid = sb("resid", [P, 2, D])
        stats = sb("stats", [P, 6])
        mv = sb("mv", [P, 2, 2])
        var = sb("var", [P, 2, 1])
        rstd = sb("rstd", [P, 2, 1])
        mhalf = sb("mhalf", [P, 1])
        x1 = sb("x1", [P, 2, ROW])
        x1T = sb("x1T", [P, 2, P])
        score, cand = sb("score", [P, E]), sb("cand", [P, E])
        top, first = sb("top", [P, 1]), sb("first", [P, 1])
        oh = sb("oh", [P, 2, E])
        cum = sb("cum", [P, E])
        place, place_oh, place_f = sb("place", [P, E]), sb("place_oh", [P, E]), sb("place_f", [P, 1])
        place_i = sb("place_i", [P, 2], I32)
        counts = sb("counts", [1, E])
        steps = sb("steps", [1, NT])
        tile_n = sb("tile_n", [1, NS])
        seq_i = sb("seq_i", [1, NT + NS], I32)
        upto = sb("upto", [1, E, E])
        cmp1, tiles = sb("cmp1", [1, E, NT]), sb("tiles", [1, E])
        cmp2, ends = sb("cmp2", [1, E, E]), sb("ends", [1, E])
        cmp3, passed = sb("cmp3", [1, NS, E]), sb("passed", [1, NS])
        cmp4, started = sb("cmp4", [1, NS, E]), sb("started", [1, NS])
        row_a, row_b = sb("row_a", [1, NS]), sb("row_b", [1, NS])
        row_i, exp_i = sb("row_i", [1, NS], I32), sb("exp_i", [1, NS], I32)
        xg = sb("xg", [P, NS * ROW])
        xs = sb("xs", [P, 2, D])
        xgT = sb("xgT", [P, 2, P])
        w1s, w2s = sb("w1s", [P, 2, W1P]), sb("w2s", [P, 2, W2P])
        hT = sb("hT", [P, 2, FC, P])
        yb, yr = sb("yb", [P, D]), sb("yr", [P, 2, D])
        ids = sb("ids", [P, 2], I32)
        ob = sb("ob", [P, 2, D])

        bank = [ctx.enter_context(nc.psum_tensor(f"bank{i}", [P, 512], F32)) for i in range(8)]
        QB, KB, XB, AB, OB, TB = bank[0], bank[1], bank[2], bank[3:5], bank[5:7], bank[7]

        l_x0, l_x = sem("l_x0"), sem("l_x")
        l_w = [sem(f"l_w{i}") for i in range(4)]
        l_moe = sem("l_moe")
        filled = sem("filled")
        c_pool, c_id = sem("c_pool"), sem("c_id")
        c_dve, c_dve1 = sem("c_dve"), sem("c_dve1")
        g_exp, g_dve, g_bc, g_use = sem("g_exp"), sem("g_dve"), sem("g_bc"), sem("g_use")
        names = """xin_ready xT_done xT_ready v_done v_ready q_done q_ready k_done k_ready sk_ready
            s0_done s1_done sl_ready max_ready sub_ready exp_ready sum_ready rrow_ready
            skt_done sk_tok_ready a0_done a1_done a_ready o_done den_ready pscale_ready pn_ready pT_ready
            pv_done att_ready attT_done attT_ready wo_done resid_ready stats_ready mv_ready var_ready
            rstd_ready x1_ready x1T_done x1T_ready rt_done score_ready top_ready cand_ready first_ready
            oh_ready rank_done place_ready place_oh_ready place_f_ready slot_ready u_done mem_ready"""
        s = {n: sem(n) for n in names.split()}
        stored = [sem("stored0"), sem("stored1")]
        n_done, sched = sem("n_done"), sem("sched")
        names = """xs_ready xgt_done xgT_ready w1s_ready w2s_ready h_done gelu_ready y_done yb_ready yr_ready
            ystats_ready ymv_ready yvar_ready yrstd_ready ob_ready ids_ready"""
        m = {n: sem(n) for n in names.split()}
        got = [sem("got0"), sem("got1")]
        sent = [sem("sent0"), sem("sent1")]

        def counted(eng, t, lo, hi):
            if isinstance(t, int):
                return lambda d: t + d + 1
            held = {d: eng.snap(t + (d + 1)) for d in range(lo, hi + 1)}
            return lambda d: held[d]

        def wait(eng, semaphore, value):
            if isinstance(value, int) and value <= 0:
                return
            eng.wait_ge(semaphore, value)

        def token_slots(eng, slot):
            for t in range(-1, 4):
                slot(t, t % 2, None)
            with eng.Fori(2, (NT - 2) // 2) as i:
                for u in range(2):
                    slot(eng.snap(i * 2 + u), u, i)
            for t in range(NT - 2, NT + 2):
                slot(t, t % 2, None)

        def tile_in(t, d):
            return not isinstance(t, int) or 0 <= t + d < NT

        def stored_value(t, u, i):
            if i is None:
                return 16 * ((t - 3) // 2 + 1)
            return i * 16 + (16 * u - 16)

        def moe_slots(eng, slot):
            for k in range(-3, 3):
                slot(k, k % 2, None)
            last = 1 + 2 * ((NS - 5) // 2)
            with eng.Fori(1, (last - 1) // 2) as i:
                for c in range(2):
                    slot(eng.snap(i * 2 + (1 + c)), 1 - c, i)
            for k in range(last, NS + 1):
                slot(k, k % 2, None)

        def moe_in(k, d):
            return not isinstance(k, int) or 0 <= k + d < NS

        def moe_value(k, d, i, c0):
            if i is None:
                return 16 * ((k + d) // 2 + 1)
            return i * 16 + 16 * ((c0 + d) // 2 + 1)

        block = ctx.enter_context(nc.Block())

        @block.sync
        def _(sp):
            xv = x.rearrange("a (t p) d -> p (a t) d", p=P)
            xd = x_sb[:, :].rearrange("p (t d) -> p t d", d=D)
            sp.dma_start(xd[:, 0:2], xv[:, 0:2]).then_inc(l_x0, 16)
            sp.dma_start(wq_sb[:, :], wq).then_inc(l_w[1], 16)
            sp.dma_start(wk_sb[:, :], wk).then_inc(l_w[1], 16)
            sp.dma_start(xd[:, 2:NT], xv[:, 2:NT]).then_inc(l_x, 16)
            sp.dma_start(w1_v[:, :, 0:F], w1.rearrange("e h f -> h e f")).then_inc(l_moe, 16)
            for e in range(E):
                sp.dma_start(w2_v[:, e, 0:FC * D].rearrange("p (c n) -> p c n", c=FC),
                             w2[e].rearrange("(c p) n -> p c n", p=P)).then_inc(l_moe, 16)
            sp.wait_ge(c_id, 5)
            for e in range(E):
                sp.dma_start(routed[e * REGION:(e + 1) * REGION, :].rearrange("(p j) c -> p (j c)", p=P).bitcast(I32),
                             fill[:, :, :].rearrange("p j c -> p (j c)")).then_inc(filled, 16)
            sp.dma_start(routed[DUMMY:DUMMY + P, :].bitcast(I32), fill[:, 0, :]).then_inc(filled, 16)
            sp.wait_ge(stored[0], 16 * (NT // 2))
            sp.wait_ge(stored[1], 16 * (NT // 2))
            sp.wait_ge(sched, 13)

            def load(k, u, i, c0):
                row = sp.value_load(row_i[0:1, bass.ds(k, 1)], min_val=0, max_val=DUMMY)
                before_it = moe_value(k, -2, i, c0)
                wait(sp, got[u], before_it)
                sp.dma_start(xg[:, bass.ds(k * ROW, ROW)], routed[bass.ds(row, P), :]).then_inc(got[u], 16)

            for k in range(3):
                load(k, k % 2, None, 0)
            with sp.Fori(1, (NS - 1) // 2) as i:
                load(sp.snap(i * 2 + 1), 1, i, 1)
                load(sp.snap(i * 2 + 2), 0, i, 2)

        @block.gpsimd
        def _(pool):
            nc.gpsimd.memset(ones[:, :], 1.0).then_inc(c_pool, 1)
            nc.gpsimd.memset(ident[:, :], 0.0).then_inc(c_pool, 1)
            pool.wait_ge(c_pool, 2)
            nc.gpsimd.affine_select(out=ident[:, :], in_=ident[:, :], compare_op=ALU.not_equal, fill=1.0, base=0,
                                    pattern=[[-1, P]], channel_multiplier=1).then_inc(c_id, 1)
            nc.gpsimd.affine_select(out=before[:, :], in_=ones[:, :], compare_op=ALU.is_gt, fill=0.0, base=0,
                                    pattern=[[1, P]], channel_multiplier=-1).then_inc(c_id, 1)
            nc.gpsimd.memset(fill[:, :, 0:D], 0).then_inc(c_id, 1)
            nc.gpsimd.iota(fill[:, :, D:ROW], [[0, NT]], base=4096, channel_multiplier=0).then_inc(c_id, 1)
            nc.gpsimd.iota(ids_i[:, :], [[P, NT]], base=0, channel_multiplier=1).then_inc(c_id, 1)
            nc.gpsimd.iota(e_i[:, :], [[1, E]], base=0, channel_multiplier=0).then_inc(c_id, 1)
            nc.gpsimd.iota(seq_i[:, 0:NT], [[P, NT]], base=0, channel_multiplier=0).then_inc(c_id, 1)
            nc.gpsimd.iota(seq_i[:, NT:NT + NS], [[1, NS]], base=0, channel_multiplier=0).then_inc(c_id, 1)
            nc.gpsimd.affine_select(out=upto[:, :, :], in_=ones[0:1, 0:E * E].rearrange("p (a b) -> p a b", a=E),
                                    compare_op=ALU.is_ge, fill=0.0, base=0, pattern=[[1, E], [-1, E]],
                                    channel_multiplier=0).then_inc(c_id, 1)

            def slot(t, u, i):
                n = counted(pool, t, -2, 1)
                w = 1 - u
                if tile_in(t, 1):
                    if isinstance(t, int) and t <= 1:
                        pool.wait_ge(l_x0 if t + 1 < 2 else l_x, 16)
                    wait(pool, s["xT_done"], n(-1))
                    nc.gpsimd.tensor_copy(xin[:, w, :], x_sb[:, bass.ds((t + 1) * D, D)]).then_inc(s["xin_ready"], 1)
                if tile_in(t, -1):
                    wait(pool, stored[w], stored_value(t, u, i))
                    nc.gpsimd.tensor_copy(x1[:, w, D:ROW].bitcast(I32), ids_i[:, bass.ds(t - 1, 1)])
                    pool.wait_ge(s["var_ready"], n(-1))
                    nc.gpsimd.tensor_tensor(rstd[:, w, :], var[:, w, :], mhalf[:, :], ALU.pow) \
                        .then_inc(s["rstd_ready"], 1)
                if tile_in(t, -2):
                    pool.wait_ge(filled, 16 * (E + 1))
                    pool.wait_ge(s["slot_ready"], n(-2))
                    nc.gpsimd.indirect_dma_start(
                        out=routed, out_offset=bass.IndirectOffsetOnAxis(ap=place_i[:, u:u + 1], axis=0),
                        in_=x1[:, u, :], in_offset=None, bounds_check=DUMMY - 1, oob_is_err=False) \
                        .then_inc(stored[u], 16)

            pool.wait_ge(c_id, 5)
            pool.wait_ge(c_dve, 3)
            token_slots(pool, slot)

            def moe(k, u, i):
                n = counted(pool, k, -1, 0)
                c0 = None if i is None else 2 - u
                if moe_in(k, 0):
                    wait(pool, sent[u], moe_value(k, -2, i, c0))
                    pool.wait_ge(m["yvar_ready"], n(0))
                    nc.gpsimd.tensor_copy(ids[:, u:u + 1], xg[:, bass.ds(k * ROW + D, 1)].bitcast(I32)) \
                        .then_inc(m["ids_ready"], 1)
                    nc.gpsimd.tensor_tensor(rstd[:, u, :], var[:, u, :], mhalf[:, :], ALU.pow) \
                        .then_inc(m["yrstd_ready"], 1)
                if moe_in(k, -1):
                    pool.wait_ge(sched, 13)
                    pool.wait_ge(m["ids_ready"], n(-1))
                    pool.wait_ge(m["ob_ready"], n(-1))
                    nc.gpsimd.indirect_dma_start(
                        out=out.rearrange("a s d -> (a s) d"),
                        out_offset=bass.IndirectOffsetOnAxis(ap=ids[:, 1 - u:2 - u], axis=0),
                        in_=ob[:, 1 - u, :], in_offset=None, bounds_check=S - 1, oob_is_err=False) \
                        .then_inc(sent[1 - u], 16)

            moe_slots(pool, moe)
            pool.wait_ge(sent[0], 16 * ((NS + 1) // 2))
            pool.wait_ge(sent[1], 16 * (NS // 2))

        @block.scalar
        def _(act):
            act.dma_start(rows_sb[:, 0:HD], betas.rearrange("a h b d -> (a b) (h d)")).then_inc(l_w[2], 16)
            act.dma_start(wv_sb[:, :], wv).then_inc(l_w[0], 16)
            act.dma_start(rows_sb[:, HD:HD + E * D], b2.rearrange("(a e) d -> a (e d)", a=1)).then_inc(l_w[2], 16)
            act.dma_start(rows_sb[:, HD + E * D:], br.rearrange("(a e) -> a e", a=1)).then_inc(l_w[2], 16)
            act.dma_start(wo_sb[:, :, :], wo.rearrange("(c p) n -> p c n", p=P)).then_inc(l_w[3], 16)
            act.dma_start(wr_sb[:, :], wr).then_inc(l_w[3], 16)
            act.dma_start(b1_rows[:, :], b1.rearrange("e (c p) -> (e c) p", p=P)).then_inc(l_w[3], 16)
            act.wait_ge(l_w[2], 48)
            nc.scalar.activation(gates_sb[:, 0:HD], rows_sb[:, 0:HD], ACT.Exp, scale=-1.0).then_inc(g_exp, 1)

            def slot(t, u, i):
                n = counted(act, t, -1, 1)
                w = 1 - u
                if tile_in(t, 0):
                    for g in range(2):
                        act.wait_ge(s[f"s{g}_done"], n(0))
                        sv = (QB, KB)[g][:, :].rearrange("p (h j) -> p h j", h=4)
                        for b in range(4):
                            r = slice(L * b, L * b + L)
                            last = nc.scalar.activation(sl[r, u, g:H:2, :], sv[r, :, L * b:L * b + L],
                                                        ACT.Copy)
                    last.then_inc(s["sl_ready"], 1)
                    act.wait_ge(s["skt_done"], n(0))
                    nc.scalar.activation(sk[:, u, :], XB[:, :], ACT.Copy).then_inc(s["sk_tok_ready"], 1)
                if tile_in(t, -1):
                    act.wait_ge(s["attT_done"], n(-1))
                    nc.scalar.activation(attT[:, w, :, :].rearrange("p c n -> p (c n)"), TB[:, :], ACT.Copy) \
                        .then_inc(s["attT_ready"], 1)
                if tile_in(t, 0):
                    act.wait_ge(s["sub_ready"], n(0))
                    nc.scalar.activation(pe_[:, u, :, :], sl[:, u, :, :], ACT.Exp, scale=SCALE) \
                        .then_inc(s["exp_ready"], 1)
                if tile_in(t, 1):
                    act.wait_ge(s["xT_done"], n(1))
                    nc.scalar.activation(xT[:, w, :], XB[:, 0:P], ACT.Copy).then_inc(s["xT_ready"], 1)
                    for c, src, raw, ex, re in (("q", QB, qT, q_exp, q_relu), ("k", KB, kT, k_exp, k_relu)):
                        act.wait_ge(s[f"{c}_done"], n(1))
                        nc.scalar.activation(raw[:, w, :, :].rearrange("p c n -> p (c n)"), src[:, :], ACT.Copy)
                        nc.scalar.activation(ex[:, :], src[:, :], ACT.Exp)
                        nc.scalar.activation(re[:, :], src[:, :], ACT.Relu).then_inc(s[f"{c}_ready"], 1)
                if tile_in(t, -1):
                    act.wait_ge(s["x1T_done"], n(-1))
                    nc.scalar.activation(x1T[:, w, :], TB[:, 0:P], ACT.Copy).then_inc(s["x1T_ready"], 1)

            token_slots(act, slot)

            def moe(k, u, i):
                n = counted(act, k, -2, 3)
                w = 1 - u
                c0 = None if i is None else 2 - u
                if moe_in(k, 1):
                    act.wait_ge(m["xgt_done"], n(1))
                    nc.scalar.activation(xgT[:, w, :], XB[:, 0:P], ACT.Copy).then_inc(m["xgT_ready"], 1)
                if moe_in(k, 0):
                    act.wait_ge(m["h_done"], n(0))
                    wait(act, m["y_done"], n(-2))
                    for c in range(FC):
                        last = nc.scalar.activation(hT[:, u, c, :], bank[u][:, c * P:(c + 1) * P], ACT.Gelu,
                                                    bias=w1s[:, u, F + c:F + c + 1])
                    last.then_inc(m["gelu_ready"], 1)
                if moe_in(k, 3):
                    act.wait_ge(got[w], moe_value(k, 3, i, c0))
                    wait(act, m["xgt_done"], n(1))
                    nc.scalar.activation(xs[:, w, :], xg[:, bass.ds((k + 3) * ROW, D)], ACT.Copy) \
                        .then_inc(m["xs_ready"], 1)
                if moe_in(k, 2):
                    e = act.value_load(exp_i[0:1, bass.ds(k + 2, 1)], min_val=0, max_val=E - 1)
                    wait(act, m["gelu_ready"], n(0))
                    nc.scalar.activation(w1s[:, u, :], w1_sb[:, bass.ds(e * W1P, W1P)], ACT.Copy) \
                        .then_inc(m["w1s_ready"], 1)

            act.wait_ge(sched, 13)
            act.wait_ge(l_moe, 16 * (E + 1))
            act.wait_ge(g_use, 6)
            moe_slots(act, moe)

        @block.tensor
        def _(pe):
            def half(h):
                return slice(DK * (h % 2), DK * (h % 2) + DK)

            pe.wait_ge(c_id, 1)
            pe.wait_ge(g_dve, 3)
            pe.wait_ge(l_w[2], 48)
            nc.tensor.matmul(AB[0][:, :], ones[0:1, :], gates_sb[:, 0:HD], start=True, stop=True).then_inc(g_bc, 1)
            nc.tensor.matmul(AB[1][:, :], ones[0:1, :], gates_sb[:, HD:2 * HD], start=True, stop=True).then_inc(g_bc, 1)
            nc.tensor.matmul(OB[0][:, :], ones[0:1, :], rows_sb[:, HD:HD + 512], start=True, stop=True).then_inc(g_bc, 1)
            nc.tensor.matmul(OB[1][:, :], ones[0:1, :], rows_sb[:, HD + 512:HD + 1024], start=True, stop=True) \
                .then_inc(g_bc, 1)
            nc.tensor.matmul(TB[:, 0:E], ones[0:1, :], rows_sb[:, HD + 1024:], start=True, stop=True).then_inc(g_bc, 1)
            pe.wait_ge(l_w[3], 48)
            nc.tensor.transpose(KB[:, 0:E * FC], b1_rows[:, :], ident[0:E * FC, 0:E * FC]).then_inc(g_bc, 1)
            pe.wait_ge(g_use, 6)
            pe.wait_ge(l_w[0], 16)
            pe.wait_ge(l_w[1], 32)
            pe.wait_ge(c_dve, 3)

            def slot(t, u, i):
                n = counted(pe, t, -2, 1)
                w = 1 - u
                if tile_in(t, -1):
                    pe.wait_ge(s["pT_ready"], n(-1))
                    for h in range(H):
                        last = nc.tensor.matmul(OB[h // 4][:, (h % 4) * V1:(h % 4) * V1 + DV], pT[:, w, h, :],
                                                vu[:, w, h, :], start=False, stop=True, skip_group_check=True)
                    last.then_inc(s["pv_done"], 1)
                if tile_in(t, 0):
                    pe.wait_ge(s["k_ready"], n(0))
                    for h in range(H):
                        p, g = h // 2, h % 2
                        last = nc.tensor.matmul((QB, KB)[g][:, p * P:(p + 1) * P], qT[half(h), u, p, :],
                                                kT[half(h), u, p, :], start=True, stop=True)
                        if p == NP - 1:
                            last.then_inc(s[f"s{g}_done"], 1)
                    pe.wait_ge(s["sk_ready"], n(0))
                    for p in range(NP):
                        last = nc.tensor.transpose(XB[:, p * P:(p + 1) * P], skT[:, u, p, :], ident[:, :])
                    last.then_inc(s["skt_done"], 1)
                if tile_in(t, -1):
                    pe.wait_ge(s["att_ready"], n(-1))
                    wait(pe, s["oh_ready"], n(-2))
                    for p in range(NP):
                        last = nc.tensor.transpose(TB[:, p * P:(p + 1) * P], att[:, w, p * P:(p + 1) * P], ident[:, :])
                    last.then_inc(s["attT_done"], 1)
                if tile_in(t, 0):
                    wait(pe, s["mem_ready"], n(-1))
                    for h in range(H):
                        p, g = h // 2, h % 2
                        last = nc.tensor.matmul(AB[g][:, p * P:(p + 1) * P], skT[half(h), u, p, :],
                                                sqT[half(h), u, p, :], start=True, stop=True)
                        if p == NP - 1:
                            last.then_inc(s[f"a{g}_done"], 1)
                if tile_in(t, -1):
                    pe.wait_ge(s["attT_ready"], n(-1))
                    for p in range(NP):
                        last = nc.tensor.matmul(TB[:, 0:D], attT[:, w, p, :], wo_sb[:, p, :],
                                                start=(p == 0), stop=(p == NP - 1))
                    last.then_inc(s["wo_done"], 1)
                if tile_in(t, 1):
                    pe.wait_ge(s["xin_ready"], n(1))
                    wait(pe, s["sk_tok_ready"], n(0))
                    nc.tensor.transpose(XB[:, 0:P], xin[:, w, :], ident[:, :]).then_inc(s["xT_done"], 1)
                if tile_in(t, 0):
                    pe.wait_ge(s["a_ready"], n(0))
                    for g in range(2):
                        for q in range(2):
                            p = 2 * g + q
                            nc.tensor.matmul(OB[g][:, q * 2 * V1:(q + 1) * 2 * V1], sqT[:, u, p, :], mem[:, u, p, :],
                                             start=(q == 0), stop=False, skip_group_check=True)
                        for h in range(4 * g, 4 * g + 4):
                            last = nc.tensor.matmul(OB[g][:, (h % 4) * V1:(h % 4 + 1) * V1], aT[:, u, h, :],
                                                    vg[:, u, h, :], start=False, stop=True, skip_group_check=True)
                    last.then_inc(s["o_done"], 1)
                if tile_in(t, -2):
                    pe.wait_ge(s["oh_ready"], n(-2))
                    nc.tensor.matmul(AB[0][:, 0:E], before[:, :], oh[:, u, :], start=True, stop=False)
                    nc.tensor.matmul(AB[0][:, 0:E], ones[:, :], cum[:, :], start=False, stop=True) \
                        .then_inc(s["rank_done"], 1)
                if tile_in(t, 1):
                    pe.wait_ge(s["xT_ready"], n(1))
                    nc.tensor.matmul(XB[:, :], xT[:, w, :], wv_sb[:, :], start=True, stop=True).then_inc(s["v_done"], 1)
                    wait(pe, s["sl_ready"], n(0))
                    for c, dst, wt in (("q", QB, wq_sb), ("k", KB, wk_sb)):
                        for p in range(NP):
                            last = nc.tensor.matmul(dst[:, p * P:(p + 1) * P], wt[:, p * P:(p + 1) * P], xT[:, w, :],
                                                    start=True, stop=True)
                        last.then_inc(s[f"{c}_done"], 1)
                if tile_in(t, -1):
                    pe.wait_ge(s["x1_ready"], n(-1))
                    nc.tensor.transpose(TB[:, 0:P], x1[:, w, 0:D], ident[:, :]).then_inc(s["x1T_done"], 1)
                if tile_in(t, 0):
                    pe.wait_ge(s["sk_tok_ready"], n(0))
                    wait(pe, s["slot_ready"], n(-2))
                    for p in range(NP):
                        last = nc.tensor.matmul(AB[p // 2][:, (p % 2) * 2 * V1:(p % 2 + 1) * 2 * V1],
                                                sk[:, u, p * P:(p + 1) * P],
                                                vg[:, u, 2 * p:2 * p + 2, :].rearrange("p h d -> p (h d)"),
                                                start=True, stop=True)
                    last.then_inc(s["u_done"], 1)
                if tile_in(t, -1):
                    pe.wait_ge(s["x1T_ready"], n(-1))
                    nc.tensor.matmul(TB[:, 256:256 + E], x1T[:, w, :], wr_sb[:, :], start=True, stop=True) \
                        .then_inc(s["rt_done"], 1)

            token_slots(pe, slot)
            pe.wait_ge(s["slot_ready"], NT)
            nc.tensor.matmul(TB[0:1, 0:E], ones[:, 0:1], cum[:, :], start=True, stop=True).then_inc(n_done, 1)

            def moe(k, u, i):
                n = counted(pe, k, -2, 2)
                w = 1 - u
                if moe_in(k, 2):
                    pe.wait_ge(m["xs_ready"], n(2))
                    wait(pe, m["xgT_ready"], n(1))
                    nc.tensor.transpose(XB[:, 0:P], xs[:, u, :], ident[:, :]).then_inc(m["xgt_done"], 1)
                if moe_in(k, 1):
                    pe.wait_ge(m["xgT_ready"], n(1))
                    pe.wait_ge(m["w1s_ready"], n(1))
                    for c in range(FC):
                        last = nc.tensor.matmul(bank[w][:, c * P:(c + 1) * P], w1s[:, w, c * P:(c + 1) * P], xgT[:, w, :],
                                                start=True, stop=True)
                    last.then_inc(m["h_done"], 1)
                if moe_in(k, 0):
                    pe.wait_ge(m["gelu_ready"], n(0))
                    pe.wait_ge(m["w2s_ready"], n(0))
                    wait(pe, m["yb_ready"], n(-2))
                    for c in range(FC):
                        last = nc.tensor.matmul(OB[u][:, 0:D], hT[:, u, c, :], w2s[:, u, c * D:(c + 1) * D],
                                                start=(c == 0), stop=(c == FC - 1))
                    last.then_inc(m["y_done"], 1)

            moe_slots(pe, moe)

        @block.vector
        def _(dve):
            V = nc.vector
            V.memset(mhalf[:, :], -0.5).then_inc(c_dve1, 1)
            V.memset(pT[:, :, :, :], 0.0).then_inc(c_dve1, 1)
            V.memset(mem[:, :, :, :], 0.0).then_inc(c_dve1, 1)
            V.memset(cum[:, :], 0.0).then_inc(c_dve1, 1)
            V.memset(vg[:, :, :, DV:V1], 1.0).then_inc(c_dve1, 1)
            for b in range(4):
                V.memset(mask[L * b:L * b + L, 0:L * (b + 1)], 0.0).then_inc(c_dve1, 1)
                if b < 3:
                    V.memset(mask[L * b:L * b + L, L * (b + 1):P], 1.0).then_inc(c_dve1, 1)
            dve.wait_ge(c_dve1, 12)
            V.memset(mem[0:DK, 0, :, DV:V1], 1.0 / DK).then_inc(c_dve, 1)
            V.memset(mem[DK:P, 0, :, V1 + DV:2 * V1], 1.0 / DK).then_inc(c_dve, 1)
            dve.wait_ge(g_exp, 1)
            V.tensor_scalar(gates_sb[:, 0:HD], gates_sb[:, 0:HD], 1.0, None, ALU.add).then_inc(g_dve, 1)
            dve.wait_ge(g_dve, 1)
            V.reciprocal(gates_sb[:, 0:HD], gates_sb[:, 0:HD]).then_inc(g_dve, 1)
            dve.wait_ge(g_dve, 2)
            V.tensor_scalar(gates_sb[:, HD:2 * HD], gates_sb[:, 0:HD], -1.0, 1.0, ALU.mult, ALU.add).then_inc(g_dve, 1)
            dve.wait_ge(c_id, 9)
            V.tensor_scalar(e_f[:, :], e_i[:, :], float(-E), None, ALU.add)
            V.tensor_copy(steps[:, :], seq_i[:, 0:NT])
            V.tensor_copy(tile_n[:, :], seq_i[:, NT:NT + NS])
            V.tensor_scalar(base_f[:, :], e_i[:, :], float(REGION), None, ALU.mult).then_inc(c_dve, 1)
            dve.wait_ge(g_bc, 6)
            V.tensor_copy(gate[:, :], AB[0][:, :]).then_inc(g_use, 1)
            V.tensor_copy(ungate[:, :], AB[1][:, :]).then_inc(g_use, 1)
            for b in range(2):
                V.tensor_copy(w2_v[:, 4 * b:4 * b + 4, FC * D:], OB[b][:, :].rearrange("p (e d) -> p e d", d=D)) \
                    .then_inc(g_use, 1)
            V.tensor_copy(br_bc[:, :], TB[:, 0:E]).then_inc(g_use, 1)
            V.tensor_copy(w1_v[:, :, F:W1P], KB[:, 0:E * FC].rearrange("p (e c) -> p e c", c=FC)).then_inc(g_use, 1)
            dve.wait_ge(g_use, 6)
            dve.wait_ge(c_dve, 3)
            dve.wait_ge(l_x0, 16)
            dve.wait_ge(l_x, 16)

            def bc(ap, *shape):
                return ap.unsqueeze(2).to_broadcast(list(shape))

            def slot(t, u, i):
                n = counted(dve, t, -2, 1)
                w = 1 - u

                def link(ins, name, d):
                    ins.then_inc(s[name], 1)
                    dve.wait_ge(s[name], n(d))

                if tile_in(t, -1):
                    dve.wait_ge(s["pv_done"], n(-1))
                    for g in range(2):
                        o = OB[g][:, 0:4 * V1].rearrange("p (h d) -> p h d", h=4)[:, :, 0:DV]
                        last = V.tensor_tensor(att[:, w, g * 256:(g + 1) * 256].rearrange("p (h d) -> p h d", h=4), o,
                                               bc(rden[:, w, 4 * g:4 * g + 4], P, 4, DV), ALU.mult)
                    last.then_inc(s["att_ready"], 1)
                if tile_in(t, -2):
                    dve.wait_ge(s["rt_done"], n(-2))
                    link(V.tensor_tensor(score[:, :], TB[:, 256:256 + E], br_bc[:, :], ALU.add), "score_ready", -2)
                    link(V.tensor_reduce(top[:, :], score[:, :], AX_X, ALU.max), "top_ready", -2)
                    link(V.scalar_tensor_tensor(out=cand[:, :], in0=score[:, :], scalar=top[:, 0:1], in1=e_f[:, :],
                                                op0=ALU.is_equal, op1=ALU.mult), "cand_ready", -2)
                    link(V.tensor_reduce(first[:, :], cand[:, :], AX_X, ALU.min), "first_ready", -2)
                    V.tensor_scalar(oh[:, u, :], e_f[:, :], first[:, 0:1], None, ALU.is_equal).then_inc(s["oh_ready"], 1)
                if tile_in(t, 0):
                    dve.wait_ge(s["sl_ready"], n(0))
                    link(V.tensor_reduce(smax[:, :], sl[:, u, :, :], AX_X, ALU.max), "max_ready", 0)
                    V.tensor_tensor(sl[:, u, :, :], sl[:, u, :, :], bc(smax[:, :], P, H, L), ALU.subtract) \
                        .then_inc(s["sub_ready"], 1)
                    for g in range(2):
                        dve.wait_ge(s[f"a{g}_done"], n(0))
                        last = V.tensor_tensor(aT[:, u, g:H:2, :], AB[g][:, :].rearrange("p (h i) -> p h i", h=4),
                                               mask[:, :].unsqueeze(1).to_broadcast([P, 4, P]), ALU.mult)
                    last.then_inc(s["a_ready"], 1)
                    dve.wait_ge(s["exp_ready"], n(0))
                    link(V.tensor_reduce(rowsum[:, :], pe_[:, u, :, :], AX_X, ALU.add), "sum_ready", 0)
                    if not tile_in(t, -1):
                        V.reciprocal(rrow[:, :], rowsum[:, :]).then_inc(s["rrow_ready"], 1)
                if tile_in(t, -1):
                    dve.wait_ge(s["wo_done"], n(-1))
                    link(V.tensor_tensor(resid[:, w, :], TB[:, 0:D], x_sb[:, bass.ds((t - 1) * D, D)], ALU.add),
                         "resid_ready", -1)
                    link(V.bn_stats(stats[:, :], resid[:, w, :]), "stats_ready", -1)
                    if tile_in(t, 0):
                        V.reciprocal(rrow[:, :], rowsum[:, :]).then_inc(s["rrow_ready"], 1)
                    link(V.bn_aggr(mv[:, w, :], stats[:, :]), "mv_ready", -1)
                    V.tensor_scalar(var[:, w, :], mv[:, w, 1:2], EPS, None, ALU.add).then_inc(s["var_ready"], 1)
                    dve.wait_ge(s["rstd_ready"], n(-1))
                    wait(dve, stored[w], stored_value(t, u, i))
                    V.tensor_scalar(x1[:, w, 0:D], resid[:, w, :], mv[:, w, 0:1], rstd[:, w, 0:1],
                                    ALU.subtract, ALU.mult).then_inc(s["x1_ready"], 1)
                if tile_in(t, 0):
                    dve.wait_ge(s["o_done"], n(0))
                    for g in range(2):
                        o = OB[g][:, 0:4 * V1].rearrange("p (h d) -> p h d", h=4)[:, :, DV]
                        last = V.tensor_copy(den[:, 4 * g:4 * g + 4], o)
                    link(last, "den_ready", 0)
                    dve.wait_ge(s["rrow_ready"], n(0))
                    V.reciprocal(rden[:, u, :], den[:, :])
                    link(V.tensor_tensor(pscale[:, :], den[:, :], rrow[:, :], ALU.mult), "pscale_ready", 0)
                    link(V.tensor_tensor(pn[:, u, :, :], pe_[:, u, :, :], bc(pscale[:, :], P, H, L), ALU.mult),
                         "pn_ready", 0)
                    for b in range(4):
                        r = slice(L * b, L * b + L)
                        last = V.transpose(pT[r, u, :, L * b:L * b + L], pn[r, u, :, :])
                    last.then_inc(s["pT_ready"], 1)
                if tile_in(t, -2):
                    dve.wait_ge(s["rank_done"], n(-2))
                    link(V.tensor_tensor(place[:, :], AB[0][:, 0:E], base_f[:, :], ALU.add), "place_ready", -2)
                    V.tensor_tensor(cum[:, :], cum[:, :], oh[:, u, :], ALU.add)
                    link(V.tensor_tensor(place_oh[:, :], place[:, :], oh[:, u, :], ALU.mult), "place_oh_ready", -2)
                    link(V.tensor_reduce(place_f[:, :], place_oh[:, :], AX_X, ALU.add), "place_f_ready", -2)
                    V.tensor_copy(place_i[:, u:u + 1], place_f[:, :]).then_inc(s["slot_ready"], 1)
                if tile_in(t, 1):
                    dve.wait_ge(s["v_done"], n(1))
                    xv = XB[:, :].rearrange("p (h d) -> p h d", h=H)
                    V.tensor_tensor(vg[:, w, :, 0:DV], xv, gate[:, :].rearrange("p (h d) -> p h d", h=H), ALU.mult)
                    V.tensor_tensor(vu[:, w, :, :], xv, ungate[:, :].rearrange("p (h d) -> p h d", h=H), ALU.mult) \
                        .then_inc(s["v_ready"], 1)
                    for c, dst, ex, re in (("q", sqT, q_exp, q_relu), ("k", skT, k_exp, k_relu)):
                        dve.wait_ge(s[f"{c}_ready"], n(1))
                        last = V.scalar_tensor_tensor(out=dst[:, w, :, :].rearrange("p c n -> p (c n)"), in0=ex[:, :],
                                                      scalar=1.0, in1=re[:, :], op0=ALU.min, op1=ALU.add)
                    last.then_inc(s["sk_ready"], 1)
                if tile_in(t, 0):
                    dve.wait_ge(s["u_done"], n(0))
                    for g in range(2):
                        for b in range(2):
                            r, c = slice(DK * b, DK * b + DK), slice(V1 * b, V1 * b + V1)
                            upd = AB[g][:, 0:4 * V1].rearrange("p (q n) -> p q n", q=2)
                            last = V.tensor_tensor(mem[r, w, 2 * g:2 * g + 2, c], upd[r, :, c],
                                                   mem[r, u, 2 * g:2 * g + 2, c], ALU.add)
                    last.then_inc(s["mem_ready"], 1)

            token_slots(dve, slot)

            did = [0]

            def step(ins):
                did[0] += 1
                ins.then_inc(sched, 1)
                dve.wait_ge(sched, did[0])

            def row3(ap, shape, axis):
                return ap.unsqueeze(axis).to_broadcast([1, *shape])

            dve.wait_ge(n_done, 1)
            step(V.tensor_copy(counts[:, :], TB[0:1, 0:E]))
            step(V.tensor_tensor(cmp1[:, :, :], row3(counts[:, :], (E, NT), 2), row3(steps[:, :], (E, NT), 1), ALU.is_gt))
            step(V.tensor_reduce(tiles[:, :], cmp1[:, :, :], AX_X, ALU.add))
            step(V.tensor_tensor(cmp2[:, :, :], row3(tiles[:, :], (E, E), 1), upto[:, :, :], ALU.mult))
            step(V.tensor_reduce(ends[:, :], cmp2[:, :, :], AX_X, ALU.add))
            step(V.tensor_tensor(cmp3[:, :, :], row3(tile_n[:, :], (NS, E), 2), row3(ends[:, :], (NS, E), 1), ALU.is_ge))
            step(V.tensor_reduce(passed[:, :], cmp3[:, :, :], AX_X, ALU.add))
            step(V.tensor_tensor(cmp4[:, :, :], cmp3[:, :, :], row3(tiles[:, :], (NS, E), 1), ALU.mult))
            step(V.tensor_reduce(started[:, :], cmp4[:, :, :], AX_X, ALU.add))
            step(V.tensor_tensor(row_a[:, :], tile_n[:, :], started[:, :], ALU.subtract))
            step(V.tensor_scalar(row_b[:, :], row_a[:, :], float(P), None, ALU.mult))
            step(V.scalar_tensor_tensor(out=row_a[:, :], in0=passed[:, :], scalar=float(REGION), in1=row_b[:, :],
                                        op0=ALU.mult, op1=ALU.add))
            V.tensor_scalar(exp_i[:, :], passed[:, :], float(E - 1), None, ALU.min)
            V.tensor_scalar(row_i[:, :], row_a[:, :], float(DUMMY), None, ALU.min).then_inc(sched, 1)
            dve.wait_ge(sched, 13)
            dve.wait_ge(l_moe, 16 * (E + 1))

            def moe(k, u, i):
                n = counted(dve, k, -2, 1)
                w = 1 - u
                c0 = None if i is None else 2 - u

                def link(ins, name):
                    ins.then_inc(m[name], 1)
                    dve.wait_ge(m[name], n(0))

                def norm():
                    dve.wait_ge(m["yrstd_ready"], n(-1))
                    wait(dve, sent[w], moe_value(k, -3, i, c0))
                    V.tensor_scalar(ob[:, w, :], yr[:, w, :], mv[:, w, 0:1], rstd[:, w, 0:1],
                                    ALU.subtract, ALU.mult).then_inc(m["ob_ready"], 1)

                if moe_in(k, 1):
                    e = dve.value_load(exp_i[0:1, bass.ds(k + 1, 1)], min_val=0, max_val=E - 1)
                    wait(dve, m["y_done"], n(-1))
                    V.tensor_copy(w2s[:, w, :], w2_sb[:, bass.ds(e * W2P, W2P)]).then_inc(m["w2s_ready"], 1)
                if moe_in(k, 0):
                    dve.wait_ge(m["y_done"], n(0))
                    link(V.tensor_tensor(yb[:, :], OB[u][:, 0:D], w2s[:, u, FC * D:W2P], ALU.add), "yb_ready")
                    link(V.tensor_tensor(yr[:, u, :], yb[:, :], xg[:, bass.ds(k * ROW, D)], ALU.add), "yr_ready")
                    link(V.bn_stats(stats[:, :], yr[:, u, :]), "ystats_ready")
                    if moe_in(k, -1):
                        norm()
                    link(V.bn_aggr(mv[:, u, :], stats[:, :]), "ymv_ready")
                    V.tensor_scalar(var[:, u, :], mv[:, u, 1:2], EPS, None, ALU.add).then_inc(m["yvar_ready"], 1)
                elif moe_in(k, -1):
                    norm()

            moe_slots(dve, moe)


_INS = ['L0_attn_x', 'L0_attn_Wq', 'L0_attn_Wk', 'L0_attn_Wv', 'L0_attn_betas', 'L0_attn_Wo', 'L0_ffn_wr', 'L0_ffn_br',
        'L0_ffn_w1', 'L0_ffn_b1', 'L0_ffn_w2', 'L0_ffn_b2']


def kernel(**inputs):
    import numpy as _np
    import concourse.bacc as _bacc
    from concourse import mybir as _mybir
    from concourse.bass_utils import run_bass_kernel_spmd as _run

    nc = _bacc.Bacc("TRN2", target_bir_lowering=False, num_devices=1)
    arrays, args = {}, []
    for name in _INS:
        a = _np.ascontiguousarray(inputs[name])
        arrays[f"in_{name}"] = a
        args.append(nc.dram_tensor(f"in_{name}", a.shape, _mybir.dt.from_np(a.dtype), kind="ExternalInput").ap())
    shape = inputs['L0_attn_x'].shape
    args.append(nc.dram_tensor("out_0", shape, _mybir.dt.float32, kind="ExternalOutput").ap())
    build_program(nc, *args)
    r = _run(nc, [arrays], core_ids=[0])
    return r.results[0]["out_0"]
```

```python
from contextlib import ExitStack

import concourse.bass as bass
from concourse import mybir

ALU = mybir.AluOpType
ACT = mybir.ActivationFunctionType
AX_X = mybir.AxisListType.X
F32 = mybir.dt.float32
I32 = mybir.dt.int32
U32 = mybir.dt.uint32

P = 128
EPS = 1e-5


def build_program(nc, x, wq, wk, wv, betas, wo, wr, br, w1, b1, w2, b2, out):
    _, S, D = x.shape
    H, DV = betas.shape[1], betas.shape[3]
    DK = wq.shape[1] // H
    L = 32
    E, _, F = w1.shape
    NT = S // P
    NP = H // 2
    HD = H * DV
    FC = F // P
    PL = P - L
    V1 = DV + 1
    NS = (S + E * (P - 1)) // P
    ROW = D + 1
    REGION = S
    DUMMY = E * REGION
    SCALE = 1.0 / float(DK) ** 0.5
    W1P = F + FC
    W2P = FC * D
    assert D == P and 2 * DK == P and DK == DV and P == 4 * L and HD == 512 and F == 512 and NT % 2 == 0
    assert S < 4096 and NS % 2 == 1

    routed = nc.dram_tensor("routed_rows", [DUMMY + P, ROW], F32).ap()

    with ExitStack() as ctx:
        def sb(name, shape, dt=F32):
            return ctx.enter_context(nc.sbuf_tensor(name, shape, dt))

        def sem(name):
            return ctx.enter_context(nc.semaphore(name))

        x_sb = sb("x_sb", [P, NT * D])
        wq_sb, wk_sb, wv_sb = sb("wq_sb", [P, 512]), sb("wk_sb", [P, 512]), sb("wv_sb", [P, 512])
        wo_sb = sb("wo_sb", [P, NP, D])
        wr_sb = sb("wr_sb", [P, E])
        w1_sb = sb("w1_sb", [P, E * W1P])
        w2_sb = sb("w2_sb", [P, E * W2P])
        b2_sb = sb("b2_sb", [P, E * D])
        w1_v = w1_sb[:, :].rearrange("p (e n) -> p e n", e=E)
        w2_v = w2_sb[:, :].rearrange("p (e n) -> p e n", e=E)
        b1_rows = sb("b1_rows", [E * FC, P])
        gate, ungate = sb("gate", [P, HD]), sb("ungate", [P, HD])
        br_bc = sb("br_bc", [P, E])
        ident = sb("ident", [P, P])
        ones = sb("ones", [P, P])
        before = sb("before", [P, P])
        mask = sb("mask", [P, P])
        ids_i = sb("ids_i", [P, NT], I32)
        e_i = sb("e_i", [P, E], I32)
        e_f = sb("e_f", [P, E])
        base_f = sb("base_f", [P, E])
        fill = sb("fill", [P, NT, ROW], I32)
        xin = sb("xin", [P, 2, D])
        xT = sb("xT", [P, 2, P])
        qT, kT = sb("qT", [P, 2, NP, P]), sb("kT", [P, 2, NP, P])
        sqT, skT = sb("sqT", [P, 2, NP, P]), sb("skT", [P, 2, NP, P])
        q_exp, q_relu = sb("q_exp", [P, HD]), sb("q_relu", [P, HD])
        k_exp, k_relu = sb("k_exp", [P, HD]), sb("k_relu", [P, HD])
        sk = sb("sk", [P, 2, HD])
        v = sb("v", [P, 2, HD])
        vg, vu = sb("vg", [P, 2, H, V1]), sb("vu", [P, 2, H, DV])
        aT = sb("aT", [P, 2, H, P])
        mem = sb("mem", [P, 2, NP, 2 * V1])
        sl, pe_, pn = sb("sl", [P, 2, H, L]), sb("pexp", [P, 2, H, L]), sb("pnorm", [P, 2, H, L])
        pblk = sb("pblk", [P, 2, H, L])
        pT = sb("pT", [P, 2, H, P])
        smax, rowsum, rrow = sb("smax", [P, H]), sb("rowsum", [P, H]), sb("rrow", [P, H])
        den, pscale = sb("den", [P, H]), sb("pscale", [P, H])
        rden = sb("rden", [P, 2, H])
        att = sb("att", [P, 2, HD])
        attT = sb("attT", [P, 2, NP, P])
        resid = sb("resid", [P, 2, D])
        stats = sb("stats", [P, 6])
        mv = sb("mv", [P, 2, 2])
        var = sb("var", [P, 2, 1])
        rstd = sb("rstd", [P, 2, 1])
        mhalf, eps = sb("mhalf", [P, 1]), sb("eps", [P, 1])
        x1 = sb("x1", [P, 2, ROW])
        x1T = sb("x1T", [P, 2, P])
        score, cand = sb("score", [P, E]), sb("cand", [P, E])
        top, first = sb("top", [P, 1]), sb("first", [P, 1])
        oh = sb("oh", [P, 2, E])
        cum = sb("cum", [P, E])
        place, place_oh, place_f = sb("place", [P, E]), sb("place_oh", [P, E]), sb("place_f", [P, 1])
        place_i = sb("place_i", [P, 2], I32)
        counts = sb("counts", [1, E])
        steps = sb("steps", [1, NT])
        tile_n = sb("tile_n", [1, NS])
        seq_i = sb("seq_i", [1, NT + NS], I32)
        upto = sb("upto", [1, E, E])
        cmp1, tiles = sb("cmp1", [1, E, NT]), sb("tiles", [1, E])
        cmp2, ends = sb("cmp2", [1, E, E]), sb("ends", [1, E])
        cmp3, passed = sb("cmp3", [1, NS, E]), sb("passed", [1, NS])
        cmp4, started = sb("cmp4", [1, NS, E]), sb("started", [1, NS])
        row_a, row_b = sb("row_a", [1, NS]), sb("row_b", [1, NS])
        row_i, exp_i = sb("row_i", [1, NS], I32), sb("exp_i", [1, NS], I32)
        xg = sb("xg", [P, NS * ROW])
        xgT = sb("xgT", [P, 2, P])
        w1s, w2s = sb("w1s", [P, 2, W1P]), sb("w2s", [P, 2, W2P])
        hT = sb("hT", [P, 2, FC, P])
        xb, yr = sb("xb", [P, 2, D]), sb("yr", [P, 2, D])
        ob = sb("ob", [P, 4, D])

        bank = [ctx.enter_context(nc.psum_tensor(f"bank{i}", [P, 512], F32)) for i in range(8)]
        QB, KB, XB, AB, OB, TB = bank[0], bank[1], bank[2], bank[3:5], bank[5:7], bank[7]

        l_x0, l_x = sem("l_x0"), sem("l_x")
        l_wv, l_wqk, l_beta, l_late = sem("l_wv"), sem("l_wqk"), sem("l_beta"), sem("l_late")
        l_moe = sem("l_moe")
        filler, filled = sem("filler"), sem("filled")
        c_pool, c_id = sem("c_pool"), sem("c_id")
        c_dve, c_dve1 = sem("c_dve"), sem("c_dve1")
        g_exp, g_dve = sem("g_exp"), sem("g_dve")
        b1_T, b1_ready = sem("b1_T"), sem("b1_ready")
        names = """xin_ready xT_done xT_ready v_done v_ready vg_ready vu_ready q_done q_ready k_done k_ready sk_ready
            s0_done s1_done sl_ready max_ready sub_ready exp_ready sum_ready rrow_ready
            skt_done sk_tok_ready a0_done a1_done a_ready o_done den_ready pscale_ready pn_ready pblk_ready pT_ready pT2_ready
            pv_done att_ready attT_done attT_ready wo_done resid_ready stats_ready mv_ready var_ready
            rstd_ready x1_ready x1T_done x1T_ready rt_done score_ready top_ready cand_ready first_ready
            oh_ready rank_done place_ready place_oh_ready place_f_ready slot_ready cum_ready u_done mem_ready"""
        s = {n: sem(n) for n in names.split()}
        stored = [sem("stored0"), sem("stored1")]
        n_done, sched = sem("n_done"), sem("sched")
        names = """xgt_done xgT_ready w1s_ready w2s_ready h_done gelu_ready y_done xb_ready yr_ready
            ystats_ready ymv_ready yvar_ready yrstd_ready ob_ready"""
        m = {n: sem(n) for n in names.split()}
        got = [sem(f"got{i}") for i in range(4)]
        sent = [sem(f"sent{i}") for i in range(4)]

        def counted(eng, t, lo, hi):
            if isinstance(t, int):
                return lambda d: t + d + 1
            held = {d: eng.snap(t + (d + 1)) for d in range(lo, hi + 1)}
            return lambda d: held[d]

        def wait(eng, semaphore, value):
            if isinstance(value, int) and value <= 0:
                return
            eng.wait_ge(semaphore, value)

        def token_slots(eng, slot):
            for t in range(-1, 4):
                slot(t, t % 2, None)
            with eng.Fori(2, (NT - 2) // 2) as i:
                for u in range(2):
                    slot(eng.snap(i * 2 + u), u, i)
            for t in range(NT - 2, NT + 2):
                slot(t, t % 2, None)

        def tile_in(t, d):
            return not isinstance(t, int) or 0 <= t + d < NT

        def stored_value(t, u, i):
            if i is None:
                return 16 * ((t - 3) // 2 + 1)
            return i * 16 + (16 * u - 16)

        def in_moe(k):
            return 0 <= k < NS

        def turns(k):
            return 16 * (k // 4 + 1)

        def set_block(copy, b, u):
            r = slice(L * b, L * b + L)
            return copy(pT[r, u, :, L * b:L * b + L], pblk[r, u, :, :])

        block = ctx.enter_context(nc.Block())

        @block.sync
        def _(sp):
            xv = x.rearrange("a (t p) d -> p (a t) d", p=P)
            xd = x_sb[:, :].rearrange("p (t d) -> p t d", d=D)
            sp.dma_start(xd[:, 0:2], xv[:, 0:2]).then_inc(l_x0, 16)
            sp.dma_start(wq_sb[:, :], wq).then_inc(l_wqk, 16)
            sp.dma_start(wk_sb[:, :], wk).then_inc(l_wqk, 16)
            sp.dma_start(xd[:, 2:NT], xv[:, 2:NT]).then_inc(l_x, 16)
            sp.dma_start(w1_v[:, :, 0:F], w1.rearrange("e h f -> h e f")).then_inc(l_moe, 16)
            for e in range(E):
                sp.dma_start(w2_v[:, e, 0:FC * D].rearrange("p (c n) -> p c n", c=FC),
                             w2[e].rearrange("(c p) n -> p c n", p=P)).then_inc(l_moe, 16)
            sp.wait_ge(filler, 2)
            for e in range(E):
                sp.dma_start(routed[e * REGION:(e + 1) * REGION, :].rearrange("(p j) c -> p (j c)", p=P).bitcast(I32),
                             fill[:, :, :].rearrange("p j c -> p (j c)")).then_inc(filled, 16)
            sp.dma_start(routed[DUMMY:DUMMY + P, :].bitcast(I32), fill[:, 0, :]).then_inc(filled, 16)
            sp.wait_ge(stored[0], 16 * (NT // 2))
            sp.wait_ge(stored[1], 16 * (NT // 2))
            sp.wait_ge(sched, 13)

            for k in range(NS):
                row = sp.value_load(row_i[0:1, k:k + 1], min_val=0, max_val=DUMMY)
                wait(sp, got[k % 4], turns(k - 4))
                sp.dma_start(xg[:, k * ROW:(k + 1) * ROW], routed[bass.ds(row, P), :]).then_inc(got[k % 4], 16)

        @block.gpsimd
        def _(pool):
            nc.gpsimd.memset(ones[:, :], 1.0).then_inc(c_pool, 1)
            nc.gpsimd.memset(ident[:, :], 0.0).then_inc(c_pool, 1)
            pool.wait_ge(c_pool, 2)
            nc.gpsimd.affine_select(out=ident[:, :], in_=ident[:, :], compare_op=ALU.not_equal, fill=1.0, base=0,
                                    pattern=[[-1, P]], channel_multiplier=1).then_inc(c_id, 1)
            pool.wait_ge(l_x0, 16)
            nc.gpsimd.tensor_copy(xin[:, 0, :], x_sb[:, 0:D]).then_inc(s["xin_ready"], 1)
            nc.gpsimd.affine_select(out=before[:, :], in_=ones[:, :], compare_op=ALU.is_gt, fill=0.0, base=0,
                                    pattern=[[1, P]], channel_multiplier=-1).then_inc(c_id, 1)
            nc.gpsimd.iota(ids_i[:, :], [[P, NT]], base=0, channel_multiplier=1).then_inc(c_id, 1)
            nc.gpsimd.iota(e_i[:, :], [[1, E]], base=0, channel_multiplier=0).then_inc(c_id, 1)
            nc.gpsimd.iota(seq_i[:, 0:NT], [[P, NT]], base=0, channel_multiplier=0).then_inc(c_id, 1)
            nc.gpsimd.iota(seq_i[:, NT:NT + NS], [[1, NS]], base=0, channel_multiplier=0).then_inc(c_id, 1)
            nc.gpsimd.affine_select(out=upto[:, :, :], in_=ones[0:1, 0:E * E].rearrange("p (a b) -> p a b", a=E),
                                    compare_op=ALU.is_ge, fill=0.0, base=0, pattern=[[1, E], [-1, E]],
                                    channel_multiplier=0).then_inc(c_id, 1)
            nc.gpsimd.iota(fill[:, :, D:ROW], [[0, NT]], base=4096, channel_multiplier=0).then_inc(filler, 1)

            def slot(t, u, i):
                n = counted(pool, t, -3, 1)
                w = 1 - u
                if tile_in(t, 1) and not (isinstance(t, int) and t < 0):
                    if isinstance(t, int) and t == 1:
                        pool.wait_ge(l_x, 16)
                    wait(pool, s["xT_done"], n(-1))
                    nc.gpsimd.tensor_copy(xin[:, w, :], x_sb[:, bass.ds((t + 1) * D, D)]).then_inc(s["xin_ready"], 1)
                if tile_in(t, -1):
                    wait(pool, stored[w], stored_value(t, u, i))
                    nc.gpsimd.tensor_copy(x1[:, w, D:ROW].bitcast(I32), ids_i[:, bass.ds(t - 1, 1)])
                    pool.wait_ge(s["mv_ready"], n(-1))
                    nc.gpsimd.tensor_tensor(var[:, w, :], mv[:, w, 1:2], eps[:, :], ALU.add).then_inc(s["var_ready"], 1)
                    pool.wait_ge(s["var_ready"], n(-1))
                    nc.gpsimd.tensor_tensor(rstd[:, w, :], var[:, w, :], mhalf[:, :], ALU.pow) \
                        .then_inc(s["rstd_ready"], 1)
                if tile_in(t, -2):
                    pool.wait_ge(filled, 16 * (E + 1))
                    pool.wait_ge(s["slot_ready"], n(-2))
                    nc.gpsimd.indirect_dma_start(
                        out=routed, out_offset=bass.IndirectOffsetOnAxis(ap=place_i[:, u:u + 1], axis=0),
                        in_=x1[:, u, :], in_offset=None, bounds_check=DUMMY - 1, oob_is_err=False) \
                        .then_inc(stored[u], 16)
                    wait(pool, s["cum_ready"], n(-3))
                    nc.gpsimd.tensor_tensor(cum[:, :], cum[:, :], oh[:, u, :], ALU.add).then_inc(s["cum_ready"], 1)
                if tile_in(t, 1):
                    pool.wait_ge(s["v_ready"], n(1))
                    nc.gpsimd.tensor_tensor(vg[:, w, :, 0:DV], v[:, w, :].rearrange("p (h d) -> p h d", h=H),
                                            gate[:, :].rearrange("p (h d) -> p h d", h=H), ALU.mult) \
                        .then_inc(s["vg_ready"], 1)

            pool.wait_ge(c_id, 7)
            pool.wait_ge(c_dve, 3)
            pool.wait_ge(g_dve, 2)
            token_slots(pool, slot)

            for k in range(NS + 1):
                u = k % 2
                if in_moe(k):
                    pool.wait_ge(m["ymv_ready"], k + 1)
                    nc.gpsimd.tensor_tensor(var[:, u, :], mv[:, u, 1:2], eps[:, :], ALU.add).then_inc(m["yvar_ready"], 1)
                    pool.wait_ge(m["yvar_ready"], k + 1)
                    nc.gpsimd.tensor_tensor(rstd[:, u, :], var[:, u, :], mhalf[:, :], ALU.pow) \
                        .then_inc(m["yrstd_ready"], 1)
                if in_moe(k - 1):
                    pool.wait_ge(m["ob_ready"], k)
                    nc.gpsimd.indirect_dma_start(
                        out=out.rearrange("a s d -> (a s) d"),
                        out_offset=bass.IndirectOffsetOnAxis(ap=xg[:, k * ROW - 1:k * ROW].bitcast(I32), axis=0),
                        in_=ob[:, (k - 1) % 4, :], in_offset=None, bounds_check=S - 1, oob_is_err=False) \
                        .then_inc(sent[(k - 1) % 4], 16)
            for j in range(4):
                pool.wait_ge(sent[j], turns(NS - 1 - (NS - 1 - j) % 4))

        @block.scalar
        def _(act):
            act.dma_start(gate[:, :], betas.rearrange("a h b d -> (a b) (h d)").to_broadcast([P, HD])) \
                .then_inc(l_beta, 16)
            act.dma_start(wv_sb[:, :], wv).then_inc(l_wv, 16)
            act.dma_start(wo_sb[:, :, :], wo.rearrange("(c p) n -> p c n", p=P)).then_inc(l_late, 16)
            act.dma_start(wr_sb[:, :], wr).then_inc(l_late, 16)
            act.dma_start(br_bc[:, :], br.rearrange("(a e) -> a e", a=1).to_broadcast([P, E])).then_inc(l_late, 16)
            act.dma_start(b1_rows[:, :], b1.rearrange("e (c p) -> (e c) p", p=P)).then_inc(l_late, 16)
            act.dma_start(b2_sb[:, :], b2.rearrange("(a e) d -> a (e d)", a=1).to_broadcast([P, E * D])) \
                .then_inc(l_moe, 16)
            act.wait_ge(l_beta, 16)
            nc.scalar.activation(gate[:, :], gate[:, :], ACT.Exp, scale=-1.0).then_inc(g_exp, 1)

            def slot(t, u, i):
                n = counted(act, t, -1, 1)
                w = 1 - u
                if tile_in(t, 0):
                    for g in range(2):
                        act.wait_ge(s[f"s{g}_done"], n(0))
                        sv = (QB, KB)[g][:, :].rearrange("p (h j) -> p h j", h=4)
                        for b in range(4):
                            r = slice(L * b, L * b + L)
                            last = nc.scalar.activation(sl[r, u, g:H:2, :], sv[r, :, L * b:L * b + L],
                                                        ACT.Copy)
                    last.then_inc(s["sl_ready"], 1)
                if tile_in(t, -1):
                    act.wait_ge(s["attT_done"], n(-1))
                    nc.scalar.activation(attT[:, w, :, :].rearrange("p c n -> p (c n)"), TB[:, :], ACT.Copy) \
                        .then_inc(s["attT_ready"], 1)
                if tile_in(t, 0):
                    act.wait_ge(s["sub_ready"], n(0))
                    nc.scalar.activation(pe_[:, u, :, :], sl[:, u, :, :], ACT.Exp, scale=SCALE) \
                        .then_inc(s["exp_ready"], 1)
                    act.wait_ge(s["skt_done"], n(0))
                    nc.scalar.activation(sk[:, u, :], XB[:, :], ACT.Copy).then_inc(s["sk_tok_ready"], 1)
                if tile_in(t, 1):
                    act.wait_ge(s["xT_done"], n(1))
                    nc.scalar.activation(xT[:, w, :], XB[:, 0:P], ACT.Copy).then_inc(s["xT_ready"], 1)
                    act.wait_ge(s["v_done"], n(1))
                    nc.scalar.activation(v[:, w, :], XB[:, :], ACT.Copy).then_inc(s["v_ready"], 1)
                if tile_in(t, 0):
                    act.wait_ge(s["pblk_ready"], n(0))
                    for b in (2, 3):
                        last = set_block(lambda o, a: nc.scalar.activation(o, a, ACT.Copy), b, u)
                    last.then_inc(s["pT2_ready"], 1)
                if tile_in(t, 1):
                    for c, src, raw, ex, re in (("q", QB, qT, q_exp, q_relu), ("k", KB, kT, k_exp, k_relu)):
                        act.wait_ge(s[f"{c}_done"], n(1))
                        nc.scalar.activation(raw[:, w, :, :].rearrange("p c n -> p (c n)"), src[:, :], ACT.Copy)
                        nc.scalar.activation(ex[:, :], src[:, :], ACT.Exp)
                        nc.scalar.activation(re[:, :], src[:, :], ACT.Relu).then_inc(s[f"{c}_ready"], 1)
                if tile_in(t, -1):
                    act.wait_ge(s["x1T_done"], n(-1))
                    nc.scalar.activation(x1T[:, w, :], TB[:, 0:P], ACT.Copy).then_inc(s["x1T_ready"], 1)

            token_slots(act, slot)

            act.wait_ge(sched, 13)
            act.wait_ge(l_moe, 16 * (E + 2))
            act.wait_ge(b1_ready, 1)
            for k in range(-2, NS):
                u, w = k % 2, 1 - k % 2
                if in_moe(k + 1):
                    act.wait_ge(m["xgt_done"], k + 2)
                    nc.scalar.activation(xgT[:, w, :], (XB, TB)[w][:, 0:P], ACT.Copy).then_inc(m["xgT_ready"], 1)
                if in_moe(k):
                    act.wait_ge(m["h_done"], k + 1)
                    wait(act, m["y_done"], k - 1)
                    for c in range(FC):
                        last = nc.scalar.activation(hT[:, u, c, :], bank[u][:, c * P:(c + 1) * P], ACT.Gelu,
                                                    bias=w1s[:, u, F + c:F + c + 1])
                    last.then_inc(m["gelu_ready"], 1)
                if in_moe(k + 2):
                    e = act.value_load(exp_i[0:1, k + 2:k + 3], min_val=0, max_val=E - 1)
                    wait(act, m["gelu_ready"], k + 1)
                    nc.scalar.activation(w1s[:, u, :], w1_sb[:, bass.ds(e * W1P, W1P)], ACT.Copy) \
                        .then_inc(m["w1s_ready"], 1)

        @block.tensor
        def _(pe):
            def half(h):
                return slice(DK * (h % 2), DK * (h % 2) + DK)

            pe.wait_ge(c_id, 1)
            pe.wait_ge(l_wv, 16)
            pe.wait_ge(l_wqk, 32)

            def slot(t, u, i):
                n = counted(pe, t, -3, 1)
                w = 1 - u
                if tile_in(t, -1):
                    pe.wait_ge(s["pT_ready"], n(-1))
                    pe.wait_ge(s["pT2_ready"], n(-1))
                    for h in range(H):
                        last = nc.tensor.matmul(OB[h // 4][:, (h % 4) * V1:(h % 4) * V1 + DV], pT[:, w, h, :],
                                                vu[:, w, h, :], start=False, stop=True, skip_group_check=True)
                    last.then_inc(s["pv_done"], 1)
                if tile_in(t, 0):
                    pe.wait_ge(s["k_ready"], n(0))
                    for h in range(H):
                        p, g = h // 2, h % 2
                        last = nc.tensor.matmul((QB, KB)[g][:, p * P:(p + 1) * P], qT[half(h), u, p, :],
                                                kT[half(h), u, p, :], start=True, stop=True)
                        if p == NP - 1:
                            last.then_inc(s[f"s{g}_done"], 1)
                if tile_in(t, -2):
                    pe.wait_ge(s["x1T_ready"], n(-2))
                    nc.tensor.matmul(TB[:, 256:256 + E], x1T[:, u, :], wr_sb[:, :], start=True, stop=True) \
                        .then_inc(s["rt_done"], 1)
                if tile_in(t, -1):
                    pe.wait_ge(s["att_ready"], n(-1))
                    wait(pe, s["score_ready"], n(-2))
                    for p in range(NP):
                        last = nc.tensor.transpose(TB[:, p * P:(p + 1) * P], att[:, w, p * P:(p + 1) * P], ident[:, :])
                    last.then_inc(s["attT_done"], 1)
                if tile_in(t, 0):
                    pe.wait_ge(s["sk_ready"], n(0))
                    wait(pe, s["mem_ready"], n(-1))
                    for h in range(H):
                        p, g = h // 2, h % 2
                        last = nc.tensor.matmul(AB[g][:, p * PL:(p + 1) * PL], skT[half(h), u, p, :],
                                                sqT[half(h), u, p, L:P], start=True, stop=True)
                        if p == NP - 1:
                            last.then_inc(s[f"a{g}_done"], 1)
                    pe.wait_ge(s["v_ready"], n(0))
                    for p in range(NP):
                        last = nc.tensor.transpose(XB[:, p * P:(p + 1) * P], skT[:, u, p, :], ident[:, :])
                    last.then_inc(s["skt_done"], 1)
                if tile_in(t, -1):
                    if isinstance(t, int) and t == 1:
                        pe.wait_ge(l_late, 64)
                    pe.wait_ge(s["attT_ready"], n(-1))
                    for p in range(NP):
                        last = nc.tensor.matmul(TB[:, 0:D], attT[:, w, p, :], wo_sb[:, p, :],
                                                start=(p == 0), stop=(p == NP - 1))
                    last.then_inc(s["wo_done"], 1)
                if tile_in(t, -2):
                    pe.wait_ge(s["oh_ready"], n(-2))
                    pe.wait_ge(s["a_ready"], NT if isinstance(t, int) and t >= NT else n(0))
                    wait(pe, s["cum_ready"], n(-3))
                    nc.tensor.matmul(AB[0][:, 0:E], before[:, :], oh[:, u, :], start=True, stop=False)
                    nc.tensor.matmul(AB[0][:, 0:E], ones[:, :], cum[:, :], start=False, stop=True) \
                        .then_inc(s["rank_done"], 1)

                def next_x():
                    pe.wait_ge(s["xin_ready"], n(1))
                    wait(pe, s["sk_tok_ready"], n(0))
                    nc.tensor.transpose(XB[:, 0:P], xin[:, w, :], ident[:, :]).then_inc(s["xT_done"], 1)

                if tile_in(t, 0):
                    pe.wait_ge(s["a_ready"], n(0))
                    pe.wait_ge(s["vg_ready"], n(0))
                    wait(pe, s["mem_ready"], n(-1))
                    for g in range(2):
                        for q in range(2):
                            p = 2 * g + q
                            nc.tensor.matmul(OB[g][:, q * 2 * V1:(q + 1) * 2 * V1], sqT[:, u, p, :], mem[:, u, p, :],
                                             start=(q == 0), stop=False, skip_group_check=True)
                        for h in range(4 * g, 4 * g + 4):
                            last = nc.tensor.matmul(OB[g][:, (h % 4) * V1:(h % 4 + 1) * V1], aT[:, u, h, :],
                                                    vg[:, u, h, :], start=False, stop=True, skip_group_check=True)
                        if g == 0 and tile_in(t, 1):
                            next_x()
                    last.then_inc(s["o_done"], 1)
                elif tile_in(t, 1):
                    next_x()
                if tile_in(t, 1):
                    pe.wait_ge(s["xT_ready"], n(1))
                    nc.tensor.matmul(XB[:, :], xT[:, w, :], wv_sb[:, :], start=True, stop=True).then_inc(s["v_done"], 1)
                    wait(pe, s["sl_ready"], n(0))
                    for c, dst, wt in (("q", QB, wq_sb), ("k", KB, wk_sb)):
                        for p in range(NP):
                            last = nc.tensor.matmul(dst[:, p * P:(p + 1) * P], wt[:, p * P:(p + 1) * P], xT[:, w, :],
                                                    start=True, stop=True)
                        last.then_inc(s[f"{c}_done"], 1)
                if tile_in(t, -1):
                    pe.wait_ge(s["x1_ready"], n(-1))
                    nc.tensor.transpose(TB[:, 0:P], x1[:, w, 0:D], ident[:, :]).then_inc(s["x1T_done"], 1)
                if tile_in(t, 0):
                    pe.wait_ge(s["sk_tok_ready"], n(0))
                    wait(pe, s["place_ready"], n(-2))
                    for p in range(NP):
                        last = nc.tensor.matmul(AB[p // 2][:, (p % 2) * 2 * V1:(p % 2 + 1) * 2 * V1],
                                                sk[:, u, p * P:(p + 1) * P],
                                                vg[:, u, 2 * p:2 * p + 2, :].rearrange("p h d -> p (h d)"),
                                                start=True, stop=True)
                    last.then_inc(s["u_done"], 1)

            token_slots(pe, slot)
            pe.wait_ge(s["cum_ready"], NT)
            nc.tensor.matmul(TB[0:1, 0:E], ones[:, 0:1], cum[:, :], start=True, stop=True).then_inc(n_done, 1)
            nc.tensor.transpose(KB[:, 0:E * FC], b1_rows[:, :], ident[0:E * FC, 0:E * FC]).then_inc(b1_T, 1)
            pe.wait_ge(sched, 13)
            for k in range(-2, NS):
                u, w = k % 2, 1 - k % 2
                if in_moe(k + 2):
                    pe.wait_ge(got[(k + 2) % 4], turns(k + 2))
                    wait(pe, m["xgT_ready"], k + 1)
                    nc.tensor.transpose((XB, TB)[u][:, 0:P], xg[:, (k + 2) * ROW:(k + 2) * ROW + D], ident[:, :]) \
                        .then_inc(m["xgt_done"], 1)
                if in_moe(k + 1):
                    pe.wait_ge(m["xgT_ready"], k + 2)
                    pe.wait_ge(m["w1s_ready"], k + 2)
                    for c in range(FC):
                        last = nc.tensor.matmul(bank[w][:, c * P:(c + 1) * P], w1s[:, w, c * P:(c + 1) * P], xgT[:, w, :],
                                                start=True, stop=True)
                    last.then_inc(m["h_done"], 1)
                if in_moe(k):
                    pe.wait_ge(m["gelu_ready"], k + 1)
                    pe.wait_ge(m["w2s_ready"], k + 1)
                    wait(pe, m["yr_ready"], k - 1)
                    for c in range(FC):
                        last = nc.tensor.matmul(OB[u][:, 0:D], hT[:, u, c, :], w2s[:, u, c * D:(c + 1) * D],
                                                start=(c == 0), stop=(c == FC - 1))
                    last.then_inc(m["y_done"], 1)

        @block.vector
        def _(dve):
            V = nc.vector
            V.memset(mhalf[:, :], -0.5).then_inc(c_dve1, 1)
            V.memset(eps[:, :], EPS).then_inc(c_dve1, 1)
            V.memset(pT[:, :, :, :], 0.0).then_inc(c_dve1, 1)
            V.memset(mem[:, :, :, :], 0.0).then_inc(c_dve1, 1)
            V.memset(cum[:, :], 0.0).then_inc(c_dve1, 1)
            V.memset(vg[:, :, :, DV:V1], 1.0).then_inc(c_dve1, 1)
            V.memset(aT[:, :, :, 0:L], 0.0).then_inc(c_dve1, 1)
            for b in range(4):
                V.memset(mask[L * b:L * b + L, 0:L * (b + 1)], 0.0).then_inc(c_dve1, 1)
                if b < 3:
                    V.memset(mask[L * b:L * b + L, L * (b + 1):P], 1.0).then_inc(c_dve1, 1)
            dve.wait_ge(c_dve1, 14)
            V.memset(mem[0:DK, 0, :, DV:V1], 1.0 / DK).then_inc(c_dve, 1)
            V.memset(mem[DK:P, 0, :, V1 + DV:2 * V1], 1.0 / DK).then_inc(c_dve, 1)
            V.memset(fill[:, :, 0:D], 0).then_inc(filler, 1)
            dve.wait_ge(g_exp, 1)
            V.tensor_scalar(ungate[:, :], gate[:, :], 1.0, None, ALU.add).then_inc(g_dve, 1)
            dve.wait_ge(g_dve, 1)
            V.reciprocal(gate[:, :], ungate[:, :]).then_inc(g_dve, 1)
            dve.wait_ge(g_dve, 2)
            V.tensor_scalar(ungate[:, :], gate[:, :], -1.0, 1.0, ALU.mult, ALU.add).then_inc(g_dve, 1)
            dve.wait_ge(c_id, 7)
            V.tensor_scalar(e_f[:, :], e_i[:, :], float(-E), None, ALU.add)
            V.tensor_copy(steps[:, :], seq_i[:, 0:NT])
            V.tensor_copy(tile_n[:, :], seq_i[:, NT:NT + NS])
            V.tensor_scalar(base_f[:, :], e_i[:, :], float(REGION), None, ALU.mult).then_inc(c_dve, 1)
            dve.wait_ge(c_dve, 3)
            dve.wait_ge(g_dve, 3)
            dve.wait_ge(l_x0, 16)
            dve.wait_ge(l_x, 16)

            def bc(ap, *shape):
                return ap.unsqueeze(2).to_broadcast(list(shape))

            def keep_earlier(g, u):
                return V.tensor_tensor(aT[:, u, g:H:2, L:P], AB[g][:, 0:4 * PL].rearrange("p (h i) -> p h i", h=4),
                                       mask[:, L:P].unsqueeze(1).to_broadcast([P, 4, PL]), ALU.mult)

            def slot(t, u, i):
                n = counted(dve, t, -2, 1)
                w = 1 - u

                def link(ins, name, d):
                    ins.then_inc(s[name], 1)
                    dve.wait_ge(s[name], n(d))

                if tile_in(t, -1):
                    dve.wait_ge(s["pv_done"], n(-1))
                    for g in range(2):
                        o = OB[g][:, 0:4 * V1].rearrange("p (h d) -> p h d", h=4)[:, :, 0:DV]
                        last = V.tensor_tensor(att[:, w, g * 256:(g + 1) * 256].rearrange("p (h d) -> p h d", h=4), o,
                                               bc(rden[:, w, 4 * g:4 * g + 4], P, 4, DV), ALU.mult)
                    last.then_inc(s["att_ready"], 1)
                cur, prv, pp = tile_in(t, 0), tile_in(t, -1), tile_in(t, -2)
                if pp:
                    if isinstance(t, int) and t == 2:
                        dve.wait_ge(l_late, 64)
                    dve.wait_ge(s["rt_done"], n(-2))
                    V.tensor_tensor(score[:, :], TB[:, 256:256 + E], br_bc[:, :], ALU.add).then_inc(s["score_ready"], 1)
                if cur:
                    dve.wait_ge(s["sl_ready"], n(0))
                    V.tensor_reduce(smax[:, :], sl[:, u, :, :], AX_X, ALU.max).then_inc(s["max_ready"], 1)
                if pp:
                    dve.wait_ge(s["score_ready"], n(-2))
                    V.tensor_reduce(top[:, :], score[:, :], AX_X, ALU.max).then_inc(s["top_ready"], 1)
                if cur:
                    dve.wait_ge(s["max_ready"], n(0))
                    V.tensor_tensor(sl[:, u, :, :], sl[:, u, :, :], bc(smax[:, :], P, H, L), ALU.subtract) \
                        .then_inc(s["sub_ready"], 1)
                if pp:
                    dve.wait_ge(s["top_ready"], n(-2))
                    V.scalar_tensor_tensor(out=cand[:, :], in0=score[:, :], scalar=top[:, 0:1], in1=e_f[:, :],
                                           op0=ALU.is_equal, op1=ALU.mult).then_inc(s["cand_ready"], 1)
                if cur:
                    dve.wait_ge(s["v_ready"], n(0))
                    V.tensor_tensor(vu[:, u, :, :].rearrange("p h d -> p (h d)"), v[:, u, :], ungate[:, :], ALU.mult) \
                        .then_inc(s["vu_ready"], 1)
                if pp:
                    dve.wait_ge(s["cand_ready"], n(-2))
                    V.tensor_reduce(first[:, :], cand[:, :], AX_X, ALU.min).then_inc(s["first_ready"], 1)
                if cur:
                    dve.wait_ge(s["a0_done"], n(0))
                    keep_earlier(0, u)
                if pp:
                    dve.wait_ge(s["first_ready"], n(-2))
                    V.tensor_scalar(oh[:, u, :], e_f[:, :], first[:, 0:1], None, ALU.is_equal).then_inc(s["oh_ready"], 1)
                if cur:
                    dve.wait_ge(s["a1_done"], n(0))
                    keep_earlier(1, u).then_inc(s["a_ready"], 1)
                    dve.wait_ge(s["exp_ready"], n(0))
                    V.tensor_reduce(rowsum[:, :], pe_[:, u, :, :], AX_X, ALU.add).then_inc(s["sum_ready"], 1)
                if prv:
                    dve.wait_ge(s["wo_done"], n(-1))
                    V.tensor_tensor(resid[:, w, :], TB[:, 0:D], x_sb[:, bass.ds((t - 1) * D, D)], ALU.add) \
                        .then_inc(s["resid_ready"], 1)
                if cur:
                    dve.wait_ge(s["sum_ready"], n(0))
                    V.reciprocal(rrow[:, :], rowsum[:, :]).then_inc(s["rrow_ready"], 1)
                if prv:
                    dve.wait_ge(s["resid_ready"], n(-1))
                    V.bn_stats(stats[:, :], resid[:, w, :]).then_inc(s["stats_ready"], 1)
                if pp:
                    dve.wait_ge(s["rank_done"], n(-2))
                    if prv:
                        dve.wait_ge(s["stats_ready"], n(-1))
                    V.tensor_tensor(place[:, :], AB[0][:, 0:E], base_f[:, :], ALU.add).then_inc(s["place_ready"], 1)
                elif prv:
                    dve.wait_ge(s["stats_ready"], n(-1))
                if prv:
                    V.bn_aggr(mv[:, w, :], stats[:, :]).then_inc(s["mv_ready"], 1)
                if pp:
                    dve.wait_ge(s["place_ready"], n(-2))
                    link(V.tensor_tensor(place_oh[:, :], place[:, :], oh[:, u, :], ALU.mult), "place_oh_ready", -2)
                    link(V.tensor_reduce(place_f[:, :], place_oh[:, :], AX_X, ALU.add), "place_f_ready", -2)
                    V.tensor_copy(place_i[:, u:u + 1], place_f[:, :]).then_inc(s["slot_ready"], 1)
                if prv:
                    dve.wait_ge(s["rstd_ready"], n(-1))
                    wait(dve, stored[w], stored_value(t, u, i))
                    V.tensor_scalar(x1[:, w, 0:D], resid[:, w, :], mv[:, w, 0:1], rstd[:, w, 0:1],
                                    ALU.subtract, ALU.mult).then_inc(s["x1_ready"], 1)
                if cur:
                    dve.wait_ge(s["o_done"], n(0))
                    for g in range(2):
                        o = OB[g][:, 0:4 * V1].rearrange("p (h d) -> p h d", h=4)[:, :, DV]
                        last = V.tensor_copy(den[:, 4 * g:4 * g + 4], o)
                    link(last, "den_ready", 0)
                    dve.wait_ge(s["rrow_ready"], n(0))
                    V.tensor_tensor(pscale[:, :], den[:, :], rrow[:, :], ALU.mult).then_inc(s["pscale_ready"], 1)
                    V.reciprocal(rden[:, u, :], den[:, :])
                    dve.wait_ge(s["pscale_ready"], n(0))
                    link(V.tensor_tensor(pn[:, u, :, :], pe_[:, u, :, :], bc(pscale[:, :], P, H, L), ALU.mult),
                         "pn_ready", 0)
                    link(V.transpose(pblk[:, u, :, :], pn[:, u, :, :]), "pblk_ready", 0)
                    set_block(V.tensor_copy, 0, u)
                    set_block(V.tensor_copy, 1, u).then_inc(s["pT_ready"], 1)
                if tile_in(t, 1):
                    for c, dst, ex, re in (("q", sqT, q_exp, q_relu), ("k", skT, k_exp, k_relu)):
                        dve.wait_ge(s[f"{c}_ready"], n(1))
                        last = V.scalar_tensor_tensor(out=dst[:, w, :, :].rearrange("p c n -> p (c n)"), in0=ex[:, :],
                                                      scalar=1.0, in1=re[:, :], op0=ALU.min, op1=ALU.add)
                    last.then_inc(s["sk_ready"], 1)
                if cur:
                    dve.wait_ge(s["u_done"], n(0))
                    for g in range(2):
                        for b in range(2):
                            r, c = slice(DK * b, DK * b + DK), slice(V1 * b, V1 * b + V1)
                            upd = AB[g][:, 0:4 * V1].rearrange("p (q n) -> p q n", q=2)
                            last = V.tensor_tensor(mem[r, w, 2 * g:2 * g + 2, c], upd[r, :, c],
                                                   mem[r, u, 2 * g:2 * g + 2, c], ALU.add)
                    last.then_inc(s["mem_ready"], 1)

            token_slots(dve, slot)

            did = [0]

            def step(ins):
                did[0] += 1
                ins.then_inc(sched, 1)
                dve.wait_ge(sched, did[0])

            def row3(ap, shape, axis):
                return ap.unsqueeze(axis).to_broadcast([1, *shape])

            dve.wait_ge(n_done, 1)
            step(V.tensor_copy(counts[:, :], TB[0:1, 0:E]))
            step(V.tensor_tensor(cmp1[:, :, :], row3(counts[:, :], (E, NT), 2), row3(steps[:, :], (E, NT), 1), ALU.is_gt))
            step(V.tensor_reduce(tiles[:, :], cmp1[:, :, :], AX_X, ALU.add))
            step(V.tensor_tensor(cmp2[:, :, :], row3(tiles[:, :], (E, E), 1), upto[:, :, :], ALU.mult))
            step(V.tensor_reduce(ends[:, :], cmp2[:, :, :], AX_X, ALU.add))
            step(V.tensor_tensor(cmp3[:, :, :], row3(tile_n[:, :], (NS, E), 2), row3(ends[:, :], (NS, E), 1), ALU.is_ge))
            step(V.tensor_reduce(passed[:, :], cmp3[:, :, :], AX_X, ALU.add))
            step(V.tensor_tensor(cmp4[:, :, :], cmp3[:, :, :], row3(tiles[:, :], (NS, E), 1), ALU.mult))
            step(V.tensor_reduce(started[:, :], cmp4[:, :, :], AX_X, ALU.add))
            step(V.tensor_tensor(row_a[:, :], tile_n[:, :], started[:, :], ALU.subtract))
            step(V.tensor_scalar(row_b[:, :], row_a[:, :], float(P), None, ALU.mult))
            step(V.scalar_tensor_tensor(out=row_a[:, :], in0=passed[:, :], scalar=float(REGION), in1=row_b[:, :],
                                        op0=ALU.mult, op1=ALU.add))
            V.tensor_scalar(exp_i[:, :], passed[:, :], float(E - 1), None, ALU.min)
            V.tensor_scalar(row_i[:, :], row_a[:, :], float(DUMMY), None, ALU.min).then_inc(sched, 1)
            dve.wait_ge(sched, 13)
            dve.wait_ge(l_moe, 16 * (E + 2))
            dve.wait_ge(b1_T, 1)
            V.tensor_copy(w1_v[:, :, F:W1P], KB[:, 0:E * FC].rearrange("p (e c) -> p e c", c=FC)).then_inc(b1_ready, 1)

            for k in range(-1, NS + 1):
                u, w = k % 2, 1 - k % 2
                if in_moe(k + 1):
                    e = dve.value_load(exp_i[0:1, k + 1:k + 2], min_val=0, max_val=E - 1)
                    wait(dve, m["y_done"], k)
                    V.tensor_copy(w2s[:, w, :], w2_sb[:, bass.ds(e * W2P, W2P)]).then_inc(m["w2s_ready"], 1)
                    dve.wait_ge(got[(k + 1) % 4], turns(k + 1))
                    V.tensor_tensor(xb[:, w, :], xg[:, (k + 1) * ROW:(k + 1) * ROW + D], b2_sb[:, bass.ds(e * D, D)],
                                    ALU.add).then_inc(m["xb_ready"], 1)
                if in_moe(k):
                    dve.wait_ge(m["y_done"], k + 1)
                    dve.wait_ge(m["xb_ready"], k + 1)
                    V.tensor_tensor(yr[:, u, :], OB[u][:, 0:D], xb[:, u, :], ALU.add).then_inc(m["yr_ready"], 1)
                if in_moe(k - 1):
                    dve.wait_ge(m["yrstd_ready"], k)
                    wait(dve, sent[(k - 1) % 4], turns(k - 5))
                    V.tensor_scalar(ob[:, (k - 1) % 4, :], yr[:, w, :], mv[:, w, 0:1], rstd[:, w, 0:1],
                                    ALU.subtract, ALU.mult).then_inc(m["ob_ready"], 1)
                if in_moe(k):
                    dve.wait_ge(m["yr_ready"], k + 1)
                    V.bn_stats(stats[:, :], yr[:, u, :]).then_inc(m["ystats_ready"], 1)
                    dve.wait_ge(m["ystats_ready"], k + 1)
                    V.bn_aggr(mv[:, u, :], stats[:, :]).then_inc(m["ymv_ready"], 1)


_INS = ['L0_attn_x', 'L0_attn_Wq', 'L0_attn_Wk', 'L0_attn_Wv', 'L0_attn_betas', 'L0_attn_Wo', 'L0_ffn_wr', 'L0_ffn_br',
        'L0_ffn_w1', 'L0_ffn_b1', 'L0_ffn_w2', 'L0_ffn_b2']


def kernel(**inputs):
    import numpy as _np
    import concourse.bacc as _bacc
    from concourse import mybir as _mybir
    from concourse.bass_utils import run_bass_kernel_spmd as _run

    nc = _bacc.Bacc("TRN2", target_bir_lowering=False, num_devices=1)
    arrays, args = {}, []
    for name in _INS:
        a = _np.ascontiguousarray(inputs[name])
        arrays[f"in_{name}"] = a
        args.append(nc.dram_tensor(f"in_{name}", a.shape, _mybir.dt.from_np(a.dtype), kind="ExternalInput").ap())
    shape = inputs['L0_attn_x'].shape
    args.append(nc.dram_tensor("out_0", shape, _mybir.dt.float32, kind="ExternalOutput").ap())
    build_program(nc, *args)
    r = _run(nc, [arrays], core_ids=[0])
    return r.results[0]["out_0"]
```

```python
from contextlib import ExitStack

import concourse.bass as bass
from concourse import mybir

ALU = mybir.AluOpType
ACT = mybir.ActivationFunctionType
AX_X = mybir.AxisListType.X
F32 = mybir.dt.float32
I32 = mybir.dt.int32
BF16 = mybir.dt.bfloat16
F32R = mybir.dt.float32r

P = 128
EPS = 1e-5


def build_program(nc, x, wq, wk, wv, betas, wo, wr, br, w1, b1, w2, b2, out):
    _, S, D = x.shape
    H, DV = betas.shape[1], betas.shape[3]
    DK = wq.shape[1] // H
    L = 32
    E, _, F = w1.shape
    NT = S // P
    NP = H // 2
    HD = H * DV
    FC = F // P
    PL = P - L
    V1 = DV + 1
    NS = (S + E * (P - 1)) // P
    ROW = D + 1
    REGION = S
    DUMMY = E * REGION
    SCALE = 1.0 / float(DK) ** 0.5
    W1P = F + FC
    W2P = FC * D
    WARM = 5
    assert D == P and 2 * DK == P and DK == DV and P == 4 * L and HD == 512 and F == 512 and NT % 2 == 0
    assert S < 4096 and NS % 2 == 1

    routed = nc.dram_tensor("routed_rows", [DUMMY + P, ROW], F32).ap()

    with ExitStack() as ctx:
        def sb(name, shape, dt=F32):
            return ctx.enter_context(nc.sbuf_tensor(name, shape, dt))

        def sem(name):
            return ctx.enter_context(nc.semaphore(name))

        x_sb = sb("x_sb", [P, NT * D])
        wq_sb, wk_sb, wv_sb = sb("wq_sb", [P, 512]), sb("wk_sb", [P, 512]), sb("wv_sb", [P, 512])
        wo_sb = sb("wo_sb", [P, NP, D])
        wr_sb = sb("wr_sb", [P, E])
        w1_sb = sb("w1_sb", [P, E * W1P])
        w2_sb = sb("w2_sb", [P, E * W2P])
        b2_sb = sb("b2_sb", [P, E * D])
        w1_v = w1_sb[:, :].rearrange("p (e n) -> p e n", e=E)
        w2_v = w2_sb[:, :].rearrange("p (e n) -> p e n", e=E)
        b1_rows = sb("b1_rows", [E * FC, P])
        gate, ungate = sb("gate", [P, HD]), sb("ungate", [P, HD])
        br_bc = sb("br_bc", [P, E])
        ident = sb("ident", [P, P])
        ones = sb("ones", [P, P])
        before = sb("before", [P, P])
        before_h, ones_h = sb("before_h", [P, P], BF16), sb("ones_h", [P, P], BF16)
        mask = sb("mask", [PL, PL])
        ids_i = sb("ids_i", [P, NT], I32)
        e_i = sb("e_i", [P, E], I32)
        e_f = sb("e_f", [P, E])
        base_f = sb("base_f", [P, E])
        fill = sb("fill", [P, NT, ROW], I32)
        xin = sb("xin", [P, 2, D])
        xT = sb("xT", [P, 2, L + P])
        qT, kT = sb("qT", [P, 2, NP, P]), sb("kT", [P, 2, NP, P])
        sqT, skT = sb("sqT", [P, 2, NP, P]), sb("skT", [P, 2, NP, P])
        q_exp, q_relu = sb("q_exp", [P, HD]), sb("q_relu", [P, HD])
        k_exp, k_relu = sb("k_exp", [P, HD]), sb("k_relu", [P, HD])
        sk = sb("sk", [P, 2, HD])
        v = sb("v", [P, 2, HD])
        vg, vu = sb("vg", [P, 2, H, V1]), sb("vu", [P, 2, H, DV])
        xh, xl = sb("xh", [P, 2, P], F32R), sb("xl", [P, 2, P], F32R)
        wvh, wvl = sb("wvh", [P, HD], F32R), sb("wvl", [P, HD], F32R)
        aT = sb("aT", [PL, 2, H, PL])
        mem = sb("mem", [P, 2, NP, 2 * V1])
        sl, pe_, pn = sb("sl", [P, 2, H, L]), sb("pexp", [P, 2, H, L]), sb("pnorm", [P, 2, H, L])
        pblk = sb("pblk", [P, 2, H, L])
        pT = sb("pT", [P, 2, H, P])
        smax, rowsum, rrow = sb("smax", [P, H]), sb("rowsum", [P, H]), sb("rrow", [P, H])
        den, pscale = sb("den", [P, H]), sb("pscale", [P, H])
        rden = sb("rden", [P, 2, H])
        att = sb("att", [P, 2, HD])
        attT = sb("attT", [P, 2, NP, P])
        resid = sb("resid", [P, 2, D])
        stats = sb("stats", [P, 6])
        mv = sb("mv", [P, 2, 2])
        var = sb("var", [P, 2, 1])
        rstd = sb("rstd", [P, 2, 1])
        mhalf, eps = sb("mhalf", [P, 1]), sb("eps", [P, 1])
        x1 = sb("x1", [P, 2, ROW])
        x1T = sb("x1T", [P, 2, P])
        score, cand = sb("score", [P, E]), sb("cand", [P, E])
        top, first = sb("top", [P, 1]), sb("first", [P, 1])
        oh = sb("oh", [P, 2, E], BF16)
        cum = sb("cum", [P, E], BF16)
        place, place_oh, place_f = sb("place", [P, E]), sb("place_oh", [P, E]), sb("place_f", [P, 1])
        place_i = sb("place_i", [P, 2], I32)
        steps = sb("steps", [1, NT])
        tile_n = sb("tile_n", [1, NS])
        seq_i = sb("seq_i", [1, NT + NS], I32)
        upto = sb("upto", [1, E, E])
        cmp1, tiles = sb("cmp1", [1, E, NT]), sb("tiles", [1, E])
        cmp2, ends = sb("cmp2", [1, E, E]), sb("ends", [1, E])
        cmp3, passed = sb("cmp3", [1, NS, E]), sb("passed", [1, NS])
        cmp4, skip, skipped = sb("cmp4", [1, NS, E]), sb("skip", [1, E]), sb("skipped", [1, NS])
        row_f = sb("row_f", [1, NS])
        row_i, exp_i = sb("row_i", [1, NS], I32), sb("exp_i", [1, NS], I32)
        xg = sb("xg", [P, NS * ROW])
        xgT = sb("xgT", [P, 2, P])
        w1s, w2s = sb("w1s", [P, 3, W1P]), sb("w2s", [P, 2, W2P])
        hT = sb("hT", [P, 2, FC, P])
        xb, yr = sb("xb", [P, 2, D]), sb("yr", [P, 2, D])
        ob = sb("ob", [P, 4, D])

        bank = [ctx.enter_context(nc.psum_tensor(f"bank{i}", [P, 512], F32)) for i in range(8)]
        RB = 4 * P - E
        QB, KB, XB, AB, OB, TB = bank[0], bank[1], bank[2], bank[3:5], bank[5:7], bank[7]

        l_x0, l_x = sem("l_x0"), sem("l_x")
        l_wq, l_wk, l_wv, l_beta, l_late = sem("l_wq"), sem("l_wk"), sem("l_wv"), sem("l_beta"), sem("l_late")
        l_moe = sem("l_moe")
        filler, cleared, filled = sem("filler"), sem("cleared"), sem("filled")
        c_pool, c_id = sem("c_pool"), sem("c_id")
        c_dve, c_dve1 = sem("c_dve"), sem("c_dve1")
        g_exp, g_dve = sem("g_exp"), sem("g_dve")
        b1_T, b1_ready = sem("b1_T"), sem("b1_ready")
        names = """xin_ready xT_done xT_ready xh_ready xl_ready v_done v_ready vg_ready vu_ready q_done q_ready k_done kt_ready k_ready sk_ready
            s0_done s1_done sl_ready max_ready sub_ready exp_ready sum_ready rrow_ready
            skt_done sk_tok_ready a0_done a1_done a_ready o_done den_ready pscale_ready pn_ready pblk_ready pT_ready pT2_ready
            pv0_done pv_done att_ready attT_done attT_ready wo_done resid_ready stats_ready mv_ready var_ready
            rstd_ready x1_ready x1T_done x1T_ready rt_done score_ready top_ready cand_ready first_ready
            oh_ready rank_done place_ready place_oh_ready place_f_ready slot_ready cum_ready u_done mem_ready"""
        s = {n: sem(n) for n in names.split()}
        stored = [sem("stored0"), sem("stored1")]
        n_done, sched = sem("n_done"), sem("sched")
        names = """xgt_done xgT_ready w1s_ready w2s_ready h_done gelu_ready y_done xb_ready yr_ready
            ystats_ready ymv_ready yvar_ready yrstd_ready ob_ready"""
        m = {n: sem(n) for n in names.split()}
        got = [sem(f"got{i}") for i in range(4)]
        sent = [sem(f"sent{i}") for i in range(4)]

        def counted(eng, t, lo, hi):
            if isinstance(t, int):
                return lambda d: t + d + 1
            held = {d: eng.snap(t + (d + 1)) for d in range(lo, hi + 1)}
            return lambda d: held[d]

        def wait(eng, semaphore, value):
            if isinstance(value, int) and value <= 0:
                return
            eng.wait_ge(semaphore, value)

        def token_slots(eng, slot):
            for t in range(-1, 4):
                slot(t, t % 2, None)
            with eng.Fori(2, (NT - 2) // 2) as i:
                for u in range(2):
                    slot(eng.snap(i * 2 + u), u, i)
            for t in range(NT - 2, NT + 2):
                slot(t, t % 2, None)

        def tile_in(t, d):
            return not isinstance(t, int) or 0 <= t + d < NT

        def stored_value(t, u, i):
            if i is None:
                return 16 * ((t - 3) // 2 + 1)
            return i * 16 + (16 * u - 16)

        def in_moe(k):
            return 0 <= k < NS

        def turns(k):
            return 16 * (k // 4 + 1)

        def set_block(copy, b, u):
            q = (b + 3) % 4 * L
            return copy(pT[L * b:L * b + L, u, :, q:q + L], pblk[q:q + L, u, :, :])

        block = ctx.enter_context(nc.Block())

        @block.sync
        def _(sp):
            xv = x.rearrange("a (t p) d -> p (a t) d", p=P)
            xd = x_sb[:, :].rearrange("p (t d) -> p t d", d=D)

            def load_x(lo, hi, semaphore):
                sp.dma_start(xd[0:PL, lo:hi], xv[L:P, lo:hi]).then_inc(semaphore, 16)
                sp.dma_start(xd[PL:P, lo:hi], xv[0:L, lo:hi]).then_inc(semaphore, 16)

            load_x(0, 1, l_x0)
            sp.dma_start(wq_sb[:, :], wq).then_inc(l_wq, 16)
            sp.dma_start(wk_sb[:, :], wk).then_inc(l_wk, 16)
            sp.dma_start(wv_sb[:, :], wv).then_inc(l_wv, 16)
            load_x(1, NT, l_x)
            sp.dma_start(wo_sb[:, :, :], wo.rearrange("(c p) n -> p c n", p=P)).then_inc(l_late, 16)
            sp.dma_start(wr_sb[:, :], wr).then_inc(l_late, 16)
            sp.dma_start(br_bc[:, :], br.rearrange("(a e) -> a e", a=1).to_broadcast([P, E])).then_inc(l_late, 16)
            sp.dma_start(b1_rows[:, :], b1.rearrange("e (c p) -> (e c) p", p=P)).then_inc(l_late, 16)
            sp.wait_ge(filler, 2)

            def clear(lo, hi, semaphore):
                n = (hi - lo) // P
                sp.dma_start(routed[lo:hi, :].rearrange("(p j) c -> p (j c)", p=P).bitcast(I32),
                             fill[:, 0:n, :].rearrange("p j c -> p (j c)")).then_inc(semaphore, 16)

            for e in range(E):
                clear(e * REGION, e * REGION + 2 * P, cleared)
            for e in range(E):
                clear(e * REGION + 2 * P, (e + 1) * REGION, filled)
            clear(DUMMY, DUMMY + P, filled)
            sp.dma_start(b2_sb[:, :], b2.rearrange("(a e) d -> a (e d)", a=1).to_broadcast([P, E * D])) \
                .then_inc(l_moe, 16)
            sp.dma_start(w1_v[:, :, 0:F], w1.rearrange("e h f -> h e f")).then_inc(l_moe, 16)
            for e in range(E):
                sp.dma_start(w2_v[:, e, 0:FC * D].rearrange("p (c n) -> p c n", c=FC),
                             w2[e].rearrange("(c p) n -> p c n", p=P)).then_inc(l_moe, 16)
            sp.wait_ge(sched, 9)
            for k in range(NS):
                row = sp.value_load(row_i[0:1, k:k + 1], min_val=0, max_val=DUMMY)
                if k == 0:
                    sp.wait_ge(stored[0], 16 * (NT // 2))
                    sp.wait_ge(stored[1], 16 * (NT // 2))
                wait(sp, got[k % 4], turns(k - 4))
                sp.dma_start(xg[:, k * ROW:(k + 1) * ROW], routed[bass.ds(row, P), :]).then_inc(got[k % 4], 16)

        @block.gpsimd
        def _(pool):
            nc.gpsimd.memset(ones[:, :], 1.0).then_inc(c_pool, 1)
            nc.gpsimd.memset(ident[:, :], 0.0).then_inc(c_pool, 1)
            pool.wait_ge(c_pool, 2)
            nc.gpsimd.affine_select(out=ident[:, :], in_=ident[:, :], compare_op=ALU.not_equal, fill=1.0, base=0,
                                    pattern=[[-1, P]], channel_multiplier=1).then_inc(c_id, 1)
            nc.gpsimd.affine_select(out=before[:, :], in_=ones[:, :], compare_op=ALU.is_gt, fill=0.0, base=0,
                                    pattern=[[1, P]], channel_multiplier=-1).then_inc(c_id, 1)
            nc.gpsimd.iota(ids_i[:, :], [[P, NT]], base=L, channel_multiplier=1).then_inc(c_id, 1)
            pool.wait_ge(c_id, 3)
            nc.gpsimd.iota(ids_i[PL:P, :], [[P, NT]], base=0, channel_multiplier=1).then_inc(c_id, 1)
            pool.wait_ge(c_id, 4)
            nc.gpsimd.iota(e_i[:, :], [[1, E]], base=0, channel_multiplier=0).then_inc(c_id, 1)
            nc.gpsimd.iota(seq_i[:, 0:NT], [[P, NT]], base=0, channel_multiplier=0).then_inc(c_id, 1)
            nc.gpsimd.iota(seq_i[:, NT:NT + NS], [[1, NS]], base=0, channel_multiplier=0).then_inc(c_id, 1)
            nc.gpsimd.affine_select(out=upto[:, :, :], in_=ones[0:1, 0:E * E].rearrange("p (a b) -> p a b", a=E),
                                    compare_op=ALU.is_ge, fill=0.0, base=0, pattern=[[1, E], [-1, E]],
                                    channel_multiplier=0).then_inc(c_id, 1)
            nc.gpsimd.memset(fill[:, :, 0:D], 0).then_inc(filler, 1)
            nc.gpsimd.iota(fill[:, :, D:ROW], [[0, NT]], base=4096, channel_multiplier=0).then_inc(filler, 1)

            def slot(t, u, i):
                n = counted(pool, t, -3, 1)
                w = 1 - u
                if tile_in(t, -1):
                    wait(pool, stored[w], stored_value(t, u, i))
                    nc.gpsimd.tensor_copy(x1[:, w, D:ROW].bitcast(I32), ids_i[:, bass.ds(t - 1, 1)])
                    pool.wait_ge(s["mv_ready"], n(-1))
                    nc.gpsimd.tensor_tensor(var[:, w, :], mv[:, w, 1:2], eps[:, :], ALU.add).then_inc(s["var_ready"], 1)
                    pool.wait_ge(s["var_ready"], n(-1))
                    nc.gpsimd.tensor_tensor(rstd[:, w, :], var[:, w, :], mhalf[:, :], ALU.pow) \
                        .then_inc(s["rstd_ready"], 1)
                if tile_in(t, -2):
                    if isinstance(t, int) and t < 4:
                        pool.wait_ge(cleared, 16 * E)
                    else:
                        pool.wait_ge(filled, 16 * (E + 1))
                    pool.wait_ge(s["slot_ready"], n(-2))
                    nc.gpsimd.indirect_dma_start(
                        out=routed, out_offset=bass.IndirectOffsetOnAxis(ap=place_i[:, u:u + 1], axis=0),
                        in_=x1[:, u, :], in_offset=None, bounds_check=DUMMY - 1, oob_is_err=False) \
                        .then_inc(stored[u], 16)
                    if not (isinstance(t, int) and t == NT + 1):
                        wait(pool, s["cum_ready"], n(-3))
                        wait(pool, s["rank_done"], n(-2))
                        nc.gpsimd.tensor_tensor(cum[:, :], cum[:, :], oh[:, u, :], ALU.add).then_inc(s["cum_ready"], 1)
                if tile_in(t, 1):
                    pool.wait_ge(s["v_ready"], n(1))
                    nc.gpsimd.tensor_tensor(vg[:, w, :, 0:DV], v[:, w, :].rearrange("p (h d) -> p h d", h=H),
                                            gate[:, :].rearrange("p (h d) -> p h d", h=H), ALU.mult) \
                        .then_inc(s["vg_ready"], 1)

            pool.wait_ge(c_id, 8)
            pool.wait_ge(c_dve1, 12)
            pool.wait_ge(g_dve, 2)
            token_slots(pool, slot)

            for k in range(NS + 1):
                u = k % 2
                if in_moe(k):
                    pool.wait_ge(m["ymv_ready"], k + 1)
                    nc.gpsimd.tensor_tensor(var[:, u, :], mv[:, u, 1:2], eps[:, :], ALU.add).then_inc(m["yvar_ready"], 1)
                    pool.wait_ge(m["yvar_ready"], k + 1)
                    nc.gpsimd.tensor_tensor(rstd[:, u, :], var[:, u, :], mhalf[:, :], ALU.pow) \
                        .then_inc(m["yrstd_ready"], 1)
                if in_moe(k - 1):
                    pool.wait_ge(m["ob_ready"], k)
                    nc.gpsimd.indirect_dma_start(
                        out=out.rearrange("a s d -> (a s) d"),
                        out_offset=bass.IndirectOffsetOnAxis(ap=xg[:, k * ROW - 1:k * ROW].bitcast(I32), axis=0),
                        in_=ob[:, (k - 1) % 4, :], in_offset=None, bounds_check=S - 1, oob_is_err=False) \
                        .then_inc(sent[(k - 1) % 4], 16)
            for j in range(4):
                pool.wait_ge(sent[j], turns(NS - 1 - (NS - 1 - j) % 4))

        @block.scalar
        def _(act):
            act.dma_start(gate[:, :], betas.rearrange("a h b d -> (a b) (h d)").to_broadcast([P, HD])) \
                .then_inc(l_beta, 16)
            act.wait_ge(c_pool, 1)
            nc.scalar.activation(q_exp[:, 0:1], ones[:, 0:1], ACT.Exp).then_inc(g_exp, 1)

            def slot(t, u, i):
                n = counted(act, t, -1, 1)
                w = 1 - u
                if tile_in(t, 1) and not (isinstance(t, int) and t < 0):
                    if isinstance(t, int) and t == 0:
                        act.wait_ge(l_x, 32)
                    wait(act, s["xT_done"], n(-1))
                    nc.scalar.activation(xin[:, w, :], x_sb[:, bass.ds((t + 1) * D, D)], ACT.Copy) \
                        .then_inc(s["xin_ready"], 1)
                if tile_in(t, 0):
                    for g in range(2):
                        act.wait_ge(s[f"s{g}_done"], n(0))
                        sv = (QB, XB)[g][:, :].rearrange("p (h j) -> p h j", h=4)
                        for b in range(4):
                            r = slice(L * b, L * b + L)
                            c = (b + 1) % 4 * L
                            last = nc.scalar.activation(sl[r, u, g:H:2, :], sv[r, :, c:c + L], ACT.Copy)
                    last.then_inc(s["sl_ready"], 1)
                if tile_in(t, -1):
                    act.wait_ge(s["attT_done"], n(-1))
                    nc.scalar.activation(attT[:, w, :, :].rearrange("p c n -> p (c n)"), TB[:, :], ACT.Copy) \
                        .then_inc(s["attT_ready"], 1)
                if tile_in(t, 1):
                    if not tile_in(t, 0):
                        act.wait_ge(l_beta, 16)
                        nc.scalar.activation(gate[:, :], gate[:, :], ACT.Exp, scale=-1.0).then_inc(g_exp, 1)
                    act.wait_ge(s["xT_done"], n(1))
                    nc.scalar.activation(xT[:, w, L:L + P], XB[:, 0:P], ACT.Copy)
                    nc.scalar.activation(xT[:, w, 0:L], XB[:, PL:P], ACT.Copy).then_inc(s["xT_ready"], 1)
                    if tile_in(t, 0):
                        act.wait_ge(s["xT_ready"], n(1))
                        nc.scalar.activation(xh[:, w, :], xT[:, w, 0:P], ACT.Copy).then_inc(s["xh_ready"], 1)
                if tile_in(t, 0):
                    act.wait_ge(s["sub_ready"], n(0))
                    nc.scalar.activation(pe_[:, u, :, :], sl[:, u, :, :], ACT.Exp, scale=SCALE) \
                        .then_inc(s["exp_ready"], 1)
                    act.wait_ge(s["skt_done"], n(0))
                    nc.scalar.activation(sk[:, u, :], KB[:, :], ACT.Copy).then_inc(s["sk_tok_ready"], 1)

                def take_v():
                    act.wait_ge(s["v_done"], n(1))
                    nc.scalar.activation(v[:, w, :], XB[:, :], ACT.Copy).then_inc(s["v_ready"], 1)

                if tile_in(t, 1):
                    if tile_in(t, 0):
                        take_v()
                    act.wait_ge(s["q_done"], n(1))
                    nc.scalar.activation(qT[:, w, :, :].rearrange("p c n -> p (c n)"), QB[:, :], ACT.Copy)
                if tile_in(t, 0):
                    act.wait_ge(s["pblk_ready"], n(0))
                    for b in (2, 3):
                        last = set_block(lambda o, a: nc.scalar.activation(o, a, ACT.Copy), b, u)
                    last.then_inc(s["pT2_ready"], 1)
                if tile_in(t, 1):
                    nc.scalar.activation(q_exp[:, :], QB[:, :], ACT.Exp)
                    nc.scalar.activation(q_relu[:, :], QB[:, :], ACT.Relu).then_inc(s["q_ready"], 1)
                    act.wait_ge(s["k_done"], n(1))
                    nc.scalar.activation(kT[:, w, :, :].rearrange("p c n -> p (c n)"), KB[:, :], ACT.Copy) \
                        .then_inc(s["kt_ready"], 1)
                    if not tile_in(t, 0):
                        take_v()
                    nc.scalar.activation(k_exp[:, :], KB[:, :], ACT.Exp)
                    nc.scalar.activation(k_relu[:, :], KB[:, :], ACT.Relu).then_inc(s["k_ready"], 1)
                if tile_in(t, -1):
                    act.wait_ge(s["x1T_done"], n(-1))
                    nc.scalar.activation(x1T[:, w, :], TB[:, 0:P], ACT.Copy).then_inc(s["x1T_ready"], 1)

            token_slots(act, slot)

            nc.scalar.activation(q_exp[:, 0:1], ones[:, 0:1], ACT.Gelu)
            act.wait_ge(sched, 9)
            act.wait_ge(l_moe, 16 * (E + 2))
            act.wait_ge(b1_ready, 1)
            e = act.value_load(exp_i[0:1, 0:1], min_val=0, max_val=E - 1)
            for k in range(-2, NS):
                u, w = k % 2, 1 - k % 2
                if in_moe(k + 1):
                    act.wait_ge(m["xgt_done"], k + 2)
                    nc.scalar.activation(xgT[:, w, :], (XB, TB)[w][:, 0:P], ACT.Copy).then_inc(m["xgT_ready"], 1)
                if in_moe(k):
                    act.wait_ge(m["h_done"], k + 1)
                    wait(act, m["y_done"], k - 1)
                    for c in range(FC):
                        last = nc.scalar.activation(hT[:, u, c, :], bank[u][:, c * P:(c + 1) * P], ACT.Gelu,
                                                    bias=w1s[:, k % 3, F + c:F + c + 1])
                    last.then_inc(m["gelu_ready"], 1)
                if in_moe(k + 2):
                    wait(act, m["gelu_ready"], k)
                    nc.scalar.activation(w1s[:, (k + 2) % 3, :], w1_sb[:, bass.ds(e * W1P, W1P)], ACT.Copy) \
                        .then_inc(m["w1s_ready"], 1)
                if in_moe(k + 3):
                    e = act.value_load(exp_i[0:1, k + 3:k + 4], min_val=0, max_val=E - 1)

        @block.tensor
        def _(pe):
            def half(h):
                return slice(DK * (h % 2), DK * (h % 2) + DK)

            pe.wait_ge(c_id, 1)

            def keep_busy(bank_, times):
                for _ in range(times):
                    nc.tensor.matmul(bank_[:, 0:P], ident[:, :], ident[:, :], start=True, stop=True)

            keep_busy(TB, WARM)

            def slot(t, u, i):
                n = counted(pe, t, -3, 1)
                w = 1 - u
                filling = isinstance(t, int) and (t == 0 or t >= NT)

                def fill_in(*times):
                    if filling:
                        keep_busy(TB if t == 0 else XB, dict(zip((0, NT, NT + 1), times))[t])

                fill_in(5, 7, 0)
                if tile_in(t, -1):
                    pe.wait_ge(s["pT_ready"], n(-1))
                    pe.wait_ge(s["pT2_ready"], n(-1))
                    for h in range(H):
                        last = nc.tensor.matmul(OB[h // 4][:, (h % 4) * V1:(h % 4) * V1 + DV], pT[:, w, h, :],
                                                vu[:, w, h, :], start=False, stop=True, skip_group_check=True)
                        if h == 3:
                            last.then_inc(s["pv0_done"], 1)
                    last.then_inc(s["pv_done"], 1)
                if tile_in(t, 0):
                    pe.wait_ge(s["kt_ready"], n(0))
                    pe.wait_ge(s["v_ready"], n(0))
                    for h in range(H):
                        p, g = h // 2, h % 2
                        last = nc.tensor.matmul((QB, XB)[g][:, p * P:(p + 1) * P], qT[half(h), u, p, :],
                                                kT[half(h), u, p, :], start=True, stop=True)
                        if p == NP - 1:
                            last.then_inc(s[f"s{g}_done"], 1)
                if tile_in(t, -2):
                    pe.wait_ge(s["x1T_ready"], n(-2))
                    pe.wait_ge(s["mem_ready"], NT - 1 if isinstance(t, int) and t >= NT else n(-1))
                    nc.tensor.matmul(AB[1][:, RB:RB + E], x1T[:, u, :], wr_sb[:, :], start=True, stop=True) \
                        .then_inc(s["rt_done"], 1)
                fill_in(0, 2, 5)
                if tile_in(t, -1):
                    pe.wait_ge(s["att_ready"], n(-1))
                    for p in range(NP):
                        last = nc.tensor.transpose(TB[:, p * P:(p + 1) * P], att[:, w, p * P:(p + 1) * P], ident[:, :])
                    last.then_inc(s["attT_done"], 1)
                def next_x():
                    if tile_in(t, 0):
                        pe.wait_ge(s["xin_ready"], n(0))
                        pe.wait_ge(s["sl_ready"], n(0))
                        rows = xin[:, w, :]
                    else:
                        pe.wait_ge(l_x0, 32)
                        rows = x_sb[:, 0:D]
                    nc.tensor.transpose(XB[:, 0:P], rows, ident[:, :]).then_inc(s["xT_done"], 1)
                    if not tile_in(t, 0):
                        keep_busy(TB, 2)

                if tile_in(t, 0):
                    pe.wait_ge(s["sk_ready"], n(0))
                    wait(pe, s["mem_ready"], n(-1))
                    wait(pe, s["score_ready"], n(-2))
                    for h in range(H):
                        p, g = h // 2, h % 2
                        last = nc.tensor.matmul(AB[g][0:PL, p * PL:(p + 1) * PL], skT[half(h), u, p, 0:PL],
                                                sqT[half(h), u, p, 0:PL], start=True, stop=True)
                        if p == NP - 1:
                            last.then_inc(s[f"a{g}_done"], 1)
                    if tile_in(t, 1):
                        next_x()
                    for p in range(NP):
                        last = nc.tensor.transpose(KB[:, p * P:(p + 1) * P], skT[:, u, p, :], ident[:, :])
                    last.then_inc(s["skt_done"], 1)
                fill_in(3, 3, 0)
                if tile_in(t, -1):
                    if isinstance(t, int) and t == 1:
                        pe.wait_ge(l_late, 64)
                    pe.wait_ge(s["attT_ready"], n(-1))
                    for p in range(NP):
                        last = nc.tensor.matmul(TB[:, 0:D], attT[:, w, p, :], wo_sb[:, p, :],
                                                start=(p == 0), stop=(p == NP - 1))
                    last.then_inc(s["wo_done"], 1)
                if tile_in(t, -2):
                    pe.wait_ge(s["oh_ready"], n(-2))
                    pe.wait_ge(s["a_ready"], NT if isinstance(t, int) and t >= NT else n(0))
                    wait(pe, s["cum_ready"], n(-3))
                    nc.tensor.matmul(AB[0][:, 0:E], before_h[:, :], oh[:, u, :], start=True, stop=False)
                    nc.tensor.matmul(AB[0][:, 0:E], ones_h[:, :], cum[:, :], start=False, stop=True) \
                        .then_inc(s["rank_done"], 1)
                    if isinstance(t, int) and t == NT + 1:
                        nc.tensor.matmul(TB[0:1, 0:E], ones_h[:, 0:1], oh[:, u, :], start=True, stop=False)
                        nc.tensor.matmul(TB[0:1, 0:E], ones_h[:, 0:1], cum[:, :], start=False, stop=True) \
                            .then_inc(n_done, 1)

                def next_v():
                    if not tile_in(t, 0):
                        nc.tensor.matmul(XB[:, :], xT[:, w, 0:P], wv_sb[:, :], start=True, stop=True) \
                            .then_inc(s["v_done"], 1)
                        return
                    if isinstance(t, int) and t == 0:
                        pe.wait_ge(g_dve, 5)
                    pe.wait_ge(s["xl_ready"], n(0))
                    nc.tensor.matmul(XB[:, :], xh[:, w, :], wvh[:, :], start=True, stop=False)
                    nc.tensor.matmul(XB[:, :], xh[:, w, :], wvl[:, :], start=False, stop=False)
                    nc.tensor.matmul(XB[:, :], xl[:, w, :], wvh[:, :], start=False, stop=True).then_inc(s["v_done"], 1)

                if tile_in(t, 0):
                    pe.wait_ge(s["a_ready"], n(0))
                    pe.wait_ge(s["vg_ready"], n(0))
                    wait(pe, s["mem_ready"], n(-1))
                    for g in range(2):
                        for q in range(2):
                            p = 2 * g + q
                            nc.tensor.matmul(OB[g][:, q * 2 * V1:(q + 1) * 2 * V1], sqT[:, u, p, :], mem[:, u, p, :],
                                             start=(q == 0), stop=False, skip_group_check=True)
                        for h in range(4 * g, 4 * g + 4):
                            last = nc.tensor.matmul(OB[g][0:PL, (h % 4) * V1:(h % 4 + 1) * V1], aT[:, u, h, :],
                                                    vg[0:PL, u, h, :], start=False, stop=True, skip_group_check=True)
                    last.then_inc(s["o_done"], 1)
                elif tile_in(t, 1):
                    next_x()
                if tile_in(t, 1):
                    pe.wait_ge(s["xT_ready"], n(1))
                    if tile_in(t, 0):
                        next_v()
                    for c, dst, wt, o in (("q", QB, wq_sb, L), ("k", KB, wk_sb, 0)):
                        if not tile_in(t, 0):
                            pe.wait_ge((l_wq, l_wk)[c == "k"], 16)
                        elif c == "k":
                            pe.wait_ge(s["sk_tok_ready"], n(0))
                        for p in range(NP):
                            last = nc.tensor.matmul(dst[:, p * P:(p + 1) * P], wt[:, p * P:(p + 1) * P], xT[:, w, o:o + P],
                                                    start=True, stop=True)
                        last.then_inc(s[f"{c}_done"], 1)
                    if not tile_in(t, 0):
                        pe.wait_ge(l_wv, 16)
                        next_v()
                if isinstance(t, int) and t == NT:
                    nc.tensor.transpose(KB[:, 0:E * FC], b1_rows[:, :], ident[0:E * FC, 0:E * FC]).then_inc(b1_T, 1)
                fill_in(0, 9, 28)
                if tile_in(t, -1):
                    pe.wait_ge(s["x1_ready"], n(-1))
                    nc.tensor.transpose(TB[:, 0:P], x1[:, w, 0:D], ident[:, :]).then_inc(s["x1T_done"], 1)
                fill_in(0, 2, 0)
                if tile_in(t, 0) and tile_in(t, 1):
                    pe.wait_ge(s["sk_tok_ready"], n(0))
                    wait(pe, s["place_ready"], n(-2))
                    for p in range(NP):
                        last = nc.tensor.matmul(AB[p // 2][:, (p % 2) * 2 * V1:(p % 2 + 1) * 2 * V1],
                                                sk[:, u, p * P:(p + 1) * P],
                                                vg[:, u, 2 * p:2 * p + 2, :].rearrange("p h d -> p (h d)"),
                                                start=True, stop=True)
                    last.then_inc(s["u_done"], 1)

            token_slots(pe, slot)
            pe.wait_ge(sched, 9)
            for k in range(-2, NS):
                u, w = k % 2, 1 - k % 2

                def turn():
                    pe.wait_ge(got[(k + 2) % 4], turns(k + 2))
                    wait(pe, m["xgT_ready"], k + 1)
                    nc.tensor.transpose((XB, TB)[u][:, 0:P], xg[:, (k + 2) * ROW:(k + 2) * ROW + D], ident[:, :]) \
                        .then_inc(m["xgt_done"], 1)

                if in_moe(k + 2) and k != -1:
                    turn()
                if in_moe(k + 1):
                    pe.wait_ge(m["xgT_ready"], k + 2)
                    pe.wait_ge(m["w1s_ready"], k + 2)
                    for c in range(FC):
                        last = nc.tensor.matmul(bank[w][:, c * P:(c + 1) * P], w1s[:, (k + 1) % 3, c * P:(c + 1) * P], xgT[:, w, :],
                                                start=True, stop=True)
                    last.then_inc(m["h_done"], 1)
                if k == -1:
                    turn()
                if in_moe(k):
                    pe.wait_ge(m["gelu_ready"], k + 1)
                    pe.wait_ge(m["w2s_ready"], k + 1)
                    wait(pe, m["yr_ready"], k - 1)
                    for c in range(FC):
                        last = nc.tensor.matmul(OB[u][:, 0:D], hT[:, u, c, :], w2s[:, u, c * D:(c + 1) * D],
                                                start=(c == 0), stop=(c == FC - 1))
                    last.then_inc(m["y_done"], 1)

        @block.vector
        def _(dve):
            V = nc.vector
            V.memset(mhalf[:, :], -0.5).then_inc(c_dve1, 1)
            V.memset(eps[:, :], EPS).then_inc(c_dve1, 1)
            V.memset(ones_h[:, :], 1.0).then_inc(c_dve1, 1)
            V.memset(pT[:, :, :, :], 0.0).then_inc(c_dve1, 1)
            V.memset(mem[:, :, :, :], 0.0).then_inc(c_dve1, 1)
            V.memset(cum[:, :], 0.0).then_inc(c_dve1, 1)
            V.memset(vg[:, :, :, DV:V1], 1.0).then_inc(c_dve1, 1)
            for b in range(3):
                V.memset(mask[L * b:L * b + L, L * b:PL], 1.0).then_inc(c_dve1, 1)
                if b > 0:
                    V.memset(mask[L * b:L * b + L, 0:L * b], 0.0).then_inc(c_dve1, 1)
            dve.wait_ge(c_dve1, 12)
            V.memset(mem[0:DK, 0, :, DV:V1], 1.0 / DK).then_inc(c_dve, 1)
            V.memset(mem[DK:P, 0, :, V1 + DV:2 * V1], 1.0 / DK).then_inc(c_dve, 1)
            dve.wait_ge(g_exp, 2)
            V.tensor_scalar(ungate[:, :], gate[:, :], 1.0, None, ALU.add).then_inc(g_dve, 1)
            dve.wait_ge(g_dve, 1)
            V.reciprocal(gate[:, :], ungate[:, :]).then_inc(g_dve, 1)

            def constants():
                V.tensor_copy(wvh[:, :], wv_sb[:, :]).then_inc(g_dve, 1)
                dve.wait_ge(g_dve, 4)
                V.tensor_tensor(wvl[:, :], wv_sb[:, :], wvh[:, :].bitcast(F32), ALU.subtract).then_inc(g_dve, 1)
                dve.wait_ge(c_id, 8)
                V.tensor_copy(before_h[:, :], before[:, :])
                V.tensor_scalar(e_f[:, :], e_i[:, :], float(-E), None, ALU.add)
                V.tensor_copy(steps[:, :], seq_i[:, 0:NT])
                V.tensor_copy(tile_n[:, :], seq_i[:, NT:NT + NS])
                V.tensor_scalar(base_f[:, :], e_i[:, :], float(REGION), None, ALU.mult).then_inc(c_dve, 1)
                dve.wait_ge(c_dve, 3)
                dve.wait_ge(l_x0, 32)
                dve.wait_ge(l_x, 32)

            def bc(ap, *shape):
                return ap.unsqueeze(2).to_broadcast(list(shape))

            def keep_earlier(g, u):
                return V.tensor_tensor(aT[:, u, g:H:2, :], AB[g][0:PL, 0:4 * PL].rearrange("p (h i) -> p h i", h=4),
                                       mask[:, :].unsqueeze(1).to_broadcast([PL, 4, PL]), ALU.mult)

            def slot(t, u, i):
                n = counted(dve, t, -2, 1)
                w = 1 - u

                def link(ins, name, d):
                    ins.then_inc(s[name], 1)
                    dve.wait_ge(s[name], n(d))

                cur, prv, pp = tile_in(t, 0), tile_in(t, -1), tile_in(t, -2)
                if pp:
                    if isinstance(t, int) and t == 2:
                        dve.wait_ge(l_late, 64)
                    dve.wait_ge(s["rt_done"], n(-2))
                    link(V.tensor_tensor(score[:, :], AB[1][:, RB:RB + E], br_bc[:, :], ALU.add), "score_ready", -2)
                    link(V.tensor_reduce(top[:, :], score[:, :], AX_X, ALU.max), "top_ready", -2)
                    link(V.scalar_tensor_tensor(out=cand[:, :], in0=score[:, :], scalar=top[:, 0:1], in1=e_f[:, :],
                                                op0=ALU.is_equal, op1=ALU.mult), "cand_ready", -2)
                    link(V.tensor_reduce(first[:, :], cand[:, :], AX_X, ALU.min), "first_ready", -2)
                    V.tensor_scalar(oh[:, u, :], e_f[:, :], first[:, 0:1], None, ALU.is_equal).then_inc(s["oh_ready"], 1)
                if cur:
                    dve.wait_ge(s["sl_ready"], n(0))
                    V.tensor_reduce(smax[:, :], sl[:, u, :, :], AX_X, ALU.max).then_inc(s["max_ready"], 1)
                    dve.wait_ge(s["a0_done"], n(0))
                    keep_earlier(0, u)
                    dve.wait_ge(s["a1_done"], n(0))
                    keep_earlier(1, u).then_inc(s["a_ready"], 1)
                    dve.wait_ge(s["max_ready"], n(0))
                    V.tensor_tensor(sl[:, u, :, :], sl[:, u, :, :], bc(smax[:, :], P, H, L), ALU.subtract) \
                        .then_inc(s["sub_ready"], 1)
                if cur and tile_in(t, 1):
                    dve.wait_ge(s["xh_ready"], n(0))
                    V.tensor_tensor(xl[:, w, :], xT[:, w, 0:P], xh[:, w, :].bitcast(F32), ALU.subtract) \
                        .then_inc(s["xl_ready"], 1)
                if isinstance(t, int) and t == 0:
                    constants()
                if prv:
                    dve.wait_ge(s["wo_done"], n(-1))
                    V.tensor_tensor(resid[:, w, :], TB[:, 0:D], x_sb[:, bass.ds((t - 1) * D, D)], ALU.add) \
                        .then_inc(s["resid_ready"], 1)
                if cur:
                    dve.wait_ge(s["exp_ready"], n(0))
                    V.tensor_reduce(rowsum[:, :], pe_[:, u, :, :], AX_X, ALU.add).then_inc(s["sum_ready"], 1)
                if cur:
                    dve.wait_ge(s["sum_ready"], n(0))
                    V.reciprocal(rrow[:, :], rowsum[:, :]).then_inc(s["rrow_ready"], 1)
                if prv:
                    dve.wait_ge(s["resid_ready"], n(-1))
                    V.bn_stats(stats[:, :], resid[:, w, :]).then_inc(s["stats_ready"], 1)
                if pp:
                    dve.wait_ge(s["rank_done"], n(-2))
                    if prv:
                        dve.wait_ge(s["stats_ready"], n(-1))
                    V.tensor_tensor(place[:, :], AB[0][:, 0:E], base_f[:, :], ALU.add).then_inc(s["place_ready"], 1)
                elif prv:
                    dve.wait_ge(s["stats_ready"], n(-1))
                if prv:
                    V.bn_aggr(mv[:, w, :], stats[:, :]).then_inc(s["mv_ready"], 1)
                if pp:
                    dve.wait_ge(s["place_ready"], n(-2))
                    link(V.tensor_tensor(place_oh[:, :], place[:, :], oh[:, u, :], ALU.mult), "place_oh_ready", -2)
                    link(V.tensor_reduce(place_f[:, :], place_oh[:, :], AX_X, ALU.add), "place_f_ready", -2)
                    V.tensor_copy(place_i[:, u:u + 1], place_f[:, :]).then_inc(s["slot_ready"], 1)
                if prv:
                    dve.wait_ge(s["rstd_ready"], n(-1))
                    wait(dve, stored[w], stored_value(t, u, i))
                    V.tensor_scalar(x1[:, w, 0:D], resid[:, w, :], mv[:, w, 0:1], rstd[:, w, 0:1],
                                    ALU.subtract, ALU.mult).then_inc(s["x1_ready"], 1)
                if cur:
                    dve.wait_ge(s["o_done"], n(0))
                    for g in range(2):
                        o = OB[g][:, 0:4 * V1].rearrange("p (h d) -> p h d", h=4)[:, :, DV]
                        last = V.tensor_copy(den[:, 4 * g:4 * g + 4], o)
                    link(last, "den_ready", 0)
                    dve.wait_ge(s["rrow_ready"], n(0))
                    V.tensor_tensor(pscale[:, :], den[:, :], rrow[:, :], ALU.mult).then_inc(s["pscale_ready"], 1)
                    V.reciprocal(rden[:, u, :], den[:, :])
                    dve.wait_ge(s["pscale_ready"], n(0))
                    link(V.tensor_tensor(pn[:, u, :, :], pe_[:, u, :, :], bc(pscale[:, :], P, H, L), ALU.mult),
                         "pn_ready", 0)
                    link(V.transpose(pblk[:, u, :, :], pn[:, u, :, :]), "pblk_ready", 0)
                    set_block(V.tensor_copy, 0, u)
                    set_block(V.tensor_copy, 1, u).then_inc(s["pT_ready"], 1)

                def sigma(c, dst, ex, re):
                    dve.wait_ge(s[f"{c}_ready"], n(1))
                    return V.scalar_tensor_tensor(out=dst[:, w, :, :].rearrange("p c n -> p (c n)"), in0=ex[:, :],
                                                  scalar=1.0, in1=re[:, :], op0=ALU.min, op1=ALU.add)

                if cur and tile_in(t, 1):
                    dve.wait_ge(s["u_done"], n(0))
                    for g in range(2):
                        for b in range(2):
                            r, c = slice(DK * b, DK * b + DK), slice(V1 * b, V1 * b + V1)
                            upd = AB[g][:, 0:4 * V1].rearrange("p (q n) -> p q n", q=2)
                            last = V.tensor_tensor(mem[r, w, 2 * g:2 * g + 2, c], upd[r, :, c],
                                                   mem[r, u, 2 * g:2 * g + 2, c], ALU.add)
                    last.then_inc(s["mem_ready"], 1)
                if tile_in(t, 1):
                    sigma("q", sqT, q_exp, q_relu)
                if cur:
                    for g in range(2):
                        dve.wait_ge(s[("pv0_done", "pv_done")[g]], n(0))
                        o = OB[g][:, 0:4 * V1].rearrange("p (h d) -> p h d", h=4)[:, :, 0:DV]
                        last = V.tensor_tensor(att[:, u, g * 256:(g + 1) * 256].rearrange("p (h d) -> p h d", h=4), o,
                                               bc(rden[:, u, 4 * g:4 * g + 4], P, 4, DV), ALU.mult)
                    last.then_inc(s["att_ready"], 1)
                if tile_in(t, 1):
                    sigma("k", skT, k_exp, k_relu).then_inc(s["sk_ready"], 1)
                if isinstance(t, int) and t < 0:
                    dve.wait_ge(g_dve, 2)
                    V.tensor_scalar(ungate[:, :], gate[:, :], -1.0, 1.0, ALU.mult, ALU.add).then_inc(g_dve, 1)
                    dve.wait_ge(l_wv, 16)
                    dve.wait_ge(g_dve, 3)
                if tile_in(t, 1):
                    dve.wait_ge(s["v_ready"], n(1))
                    V.tensor_tensor(vu[:, w, :, :].rearrange("p h d -> p (h d)"), v[:, w, :], ungate[:, :], ALU.mult) \
                        .then_inc(s["vu_ready"], 1)

            token_slots(dve, slot)

            did = [0]

            def step(ins):
                did[0] += 1
                ins.then_inc(sched, 1)
                dve.wait_ge(sched, did[0])

            def row3(ap, shape, axis):
                return ap.unsqueeze(axis).to_broadcast([1, *shape])

            dve.wait_ge(l_moe, 16 * (E + 2))
            dve.wait_ge(b1_T, 1)
            V.tensor_copy(w1_v[:, :, F:W1P], KB[:, 0:E * FC].rearrange("p (e c) -> p e c", c=FC)).then_inc(b1_ready, 1)
            dve.wait_ge(n_done, 1)
            step(V.tensor_tensor(cmp1[:, :, :], row3(TB[0:1, 0:E], (E, NT), 2), row3(steps[:, :], (E, NT), 1), ALU.is_gt))
            step(V.tensor_reduce(tiles[:, :], cmp1[:, :, :], AX_X, ALU.add))
            V.tensor_scalar(skip[:, :], tiles[:, :], -float(P), float(REGION), ALU.mult, ALU.add)
            step(V.tensor_tensor(cmp2[:, :, :], row3(tiles[:, :], (E, E), 1), upto[:, :, :], ALU.mult))
            step(V.tensor_reduce(ends[:, :], cmp2[:, :, :], AX_X, ALU.add))
            step(V.tensor_tensor(cmp3[:, :, :], row3(tile_n[:, :], (NS, E), 2), row3(ends[:, :], (NS, E), 1), ALU.is_ge))
            V.tensor_reduce(passed[:, :], cmp3[:, :, :], AX_X, ALU.add)
            step(V.tensor_tensor(cmp4[:, :, :], cmp3[:, :, :], row3(skip[:, :], (NS, E), 1), ALU.mult))
            V.tensor_scalar(exp_i[:, :], passed[:, :], float(E - 1), None, ALU.min)
            step(V.tensor_reduce(skipped[:, :], cmp4[:, :, :], AX_X, ALU.add))
            step(V.scalar_tensor_tensor(out=row_f[:, :], in0=tile_n[:, :], scalar=float(P), in1=skipped[:, :],
                                        op0=ALU.mult, op1=ALU.add))
            step(V.tensor_scalar(row_i[:, :], row_f[:, :], float(DUMMY), None, ALU.min))

            e = dve.value_load(exp_i[0:1, 0:1], min_val=0, max_val=E - 1)
            for k in range(-1, NS + 1):
                u, w = k % 2, 1 - k % 2
                if in_moe(k + 1):
                    wait(dve, m["y_done"], k)
                    V.tensor_copy(w2s[:, w, :], w2_sb[:, bass.ds(e * W2P, W2P)]).then_inc(m["w2s_ready"], 1)
                    dve.wait_ge(got[(k + 1) % 4], turns(k + 1))
                    V.tensor_tensor(xb[:, w, :], xg[:, (k + 1) * ROW:(k + 1) * ROW + D], b2_sb[:, bass.ds(e * D, D)],
                                    ALU.add).then_inc(m["xb_ready"], 1)
                if in_moe(k + 2):
                    e = dve.value_load(exp_i[0:1, k + 2:k + 3], min_val=0, max_val=E - 1)
                if in_moe(k):
                    dve.wait_ge(m["y_done"], k + 1)
                    dve.wait_ge(m["xb_ready"], k + 1)
                    V.tensor_tensor(yr[:, u, :], OB[u][:, 0:D], xb[:, u, :], ALU.add).then_inc(m["yr_ready"], 1)
                if in_moe(k - 1):
                    dve.wait_ge(m["yrstd_ready"], k)
                    wait(dve, sent[(k - 1) % 4], turns(k - 5))
                    V.tensor_scalar(ob[:, (k - 1) % 4, :], yr[:, w, :], mv[:, w, 0:1], rstd[:, w, 0:1],
                                    ALU.subtract, ALU.mult).then_inc(m["ob_ready"], 1)
                if in_moe(k):
                    dve.wait_ge(m["yr_ready"], k + 1)
                    V.bn_stats(stats[:, :], yr[:, u, :]).then_inc(m["ystats_ready"], 1)
                    dve.wait_ge(m["ystats_ready"], k + 1)
                    V.bn_aggr(mv[:, u, :], stats[:, :]).then_inc(m["ymv_ready"], 1)


_INS = ['L0_attn_x', 'L0_attn_Wq', 'L0_attn_Wk', 'L0_attn_Wv', 'L0_attn_betas', 'L0_attn_Wo', 'L0_ffn_wr', 'L0_ffn_br',
        'L0_ffn_w1', 'L0_ffn_b1', 'L0_ffn_w2', 'L0_ffn_b2']


def kernel(**inputs):
    import numpy as _np
    import concourse.bacc as _bacc
    from concourse import mybir as _mybir
    from concourse.bass_utils import run_bass_kernel_spmd as _run

    nc = _bacc.Bacc("TRN2", target_bir_lowering=False, num_devices=1)
    arrays, args = {}, []
    for name in _INS:
        a = _np.ascontiguousarray(inputs[name])
        arrays[f"in_{name}"] = a
        args.append(nc.dram_tensor(f"in_{name}", a.shape, _mybir.dt.from_np(a.dtype), kind="ExternalInput").ap())
    shape = inputs['L0_attn_x'].shape
    args.append(nc.dram_tensor("out_0", shape, _mybir.dt.float32, kind="ExternalOutput").ap())
    build_program(nc, *args)
    r = _run(nc, [arrays], core_ids=[0])
    return r.results[0]["out_0"]
```
